# Optimizing a Trainium2 kernel written in Bass

```python
import numpy as np
import jax
import jax.numpy as jnp

def _softmax(x, axis=-1):
    return jax.nn.softmax(x, axis=axis)

def _gelu(x):
    return jax.nn.gelu(x, approximate=True)

def _silu(x):
    return jax.nn.silu(x)

def _sigmoid(x):
    return jax.nn.sigmoid(x)

def _layernorm(x, axis=-1, eps=1e-05):
    m = jnp.mean(x, axis=axis, keepdims=True)
    v = jnp.var(x, axis=axis, keepdims=True)
    return (x - m) / jnp.sqrt(v + eps)

def _scatter_add(tgt, idx, src, axis=0):
    return tgt.at[idx].add(src)

def _segment_sum(src, seg, n):
    return jax.ops.segment_sum(src, seg, n)
kernel_name = 'mk_adaln_d1_jaxref_r8_b8add2'

def setup_inputs(seed: int=0):
    np.random.seed(seed)
    _w = jnp.asarray

    def _L0_attn_setup():
        import jax, jax.numpy as jnp
        import numpy as np
        B, T, D, N, R = (2, 256, 128, 16, 64)
        key = jax.random.key(seed)
        ks = jax.random.split(key, 8)
        sc = 0.02
        return {'x': jax.random.normal(ks[0], (B, T, D), jnp.float32), 'W_in': jax.random.normal(ks[1], (2 * D, D), jnp.float32) * sc, 'conv_w': jax.random.normal(ks[2], (D, 3), jnp.float32) * sc, 'W_x': jax.random.normal(ks[3], (R + 2 * N, D), jnp.float32) * sc, 'W_dt': jax.random.normal(ks[4], (D, R), jnp.float32) * sc, 'b_dt': jnp.ones((D,), jnp.float32), 'A_log': jnp.full((D, N), -2.0, jnp.float32), 'D_param': jnp.ones((D,), jnp.float32), 'W_C': jax.random.normal(ks[5], (D, N), jnp.float32) * sc, 'W_out': jax.random.normal(ks[6], (D, D), jnp.float32) * sc}
    _L0_attn_in = _L0_attn_setup()

    def _L0_ffn_setup():
        import jax, jax.numpy as jnp
        import numpy as np
        D_MODEL = 128
        HIDDEN = 512
        N_ROUTING = 2
        key = jax.random.key(seed)
        ks = jax.random.split(key, 10)
        s = 0.02
        x = jax.random.normal(ks[0], (4, 512, D_MODEL), dtype=jnp.float32)
        gate_w = jax.random.normal(ks[1], (N_ROUTING, D_MODEL), dtype=jnp.float32) * s
        w1 = jax.random.normal(ks[2], (N_ROUTING, D_MODEL, HIDDEN), dtype=jnp.float32) * s
        b1 = jax.random.normal(ks[3], (N_ROUTING, HIDDEN), dtype=jnp.float32) * s
        w2 = jax.random.normal(ks[4], (N_ROUTING, HIDDEN, D_MODEL), dtype=jnp.float32) * s
        b2 = jax.random.normal(ks[5], (N_ROUTING, D_MODEL), dtype=jnp.float32) * s
        sw1 = jax.random.normal(ks[6], (D_MODEL, HIDDEN), dtype=jnp.float32) * s
        sb1 = jax.random.normal(ks[7], (HIDDEN,), dtype=jnp.float32) * s
        sw2 = jax.random.normal(ks[8], (HIDDEN, D_MODEL), dtype=jnp.float32) * s
        sb2 = jax.random.normal(ks[9], (D_MODEL,), dtype=jnp.float32) * s
        return {'x': x, 'gate_w': gate_w, 'w1': w1, 'b1': b1, 'w2': w2, 'b2': b2, 'sw1': sw1, 'sb1': sb1, 'sw2': sw2, 'sb2': sb2}
    _L0_ffn_in = _L0_ffn_setup()
    _L0_c = _w((lambda *s: np.random.randn(*s).astype(np.float32) * 0.05)(8, 128))
    _L0_wmod = _w((lambda *s: np.random.randn(*s).astype(np.float32) * 0.05)(128, 6 * 128) * 128 ** (-0.5))
    _d = {'L0_attn_x': _L0_attn_in['x'], 'L0_attn_W_in': _L0_attn_in['W_in'], 'L0_attn_conv_w': _L0_attn_in['conv_w'], 'L0_attn_W_x': _L0_attn_in['W_x'], 'L0_attn_W_dt': _L0_attn_in['W_dt'], 'L0_attn_b_dt': _L0_attn_in['b_dt'], 'L0_attn_A_log': _L0_attn_in['A_log'], 'L0_attn_D_param': _L0_attn_in['D_param'], 'L0_attn_W_C': _L0_attn_in['W_C'], 'L0_attn_W_out': _L0_attn_in['W_out'], 'L0_ffn_gate_w': _L0_ffn_in['gate_w'], 'L0_ffn_w1': _L0_ffn_in['w1'], 'L0_ffn_b1': _L0_ffn_in['b1'], 'L0_ffn_w2': _L0_ffn_in['w2'], 'L0_ffn_b2': _L0_ffn_in['b2'], 'L0_ffn_sw1': _L0_ffn_in['sw1'], 'L0_ffn_sb1': _L0_ffn_in['sb1'], 'L0_ffn_sw2': _L0_ffn_in['sw2'], 'L0_ffn_sb2': _L0_ffn_in['sb2'], 'L0_c': _L0_c, 'L0_wmod': _L0_wmod}
    _x0 = _d['L0_attn_x']
    _d['L0_attn_x'] = jax.random.normal(jax.random.fold_in(jax.random.key(seed), 1), (8, 512, 128), dtype=_x0.dtype)
    del _x0
    return _d

def reference(L0_attn_x, L0_attn_W_in, L0_attn_conv_w, L0_attn_W_x, L0_attn_W_dt, L0_attn_b_dt, L0_attn_A_log, L0_attn_D_param, L0_attn_W_C, L0_attn_W_out, L0_ffn_gate_w, L0_ffn_w1, L0_ffn_b1, L0_ffn_w2, L0_ffn_b2, L0_ffn_sw1, L0_ffn_sb1, L0_ffn_sw2, L0_ffn_sb2, L0_c, L0_wmod):

    def _L0_attn_ref(x, W_in, conv_w, W_x, W_dt, b_dt, A_log, D_param, W_C, W_out):
        import jax, jax.numpy as jnp
        import numpy as np
        B, T, D, N, R = (2, 256, 128, 16, 64)
        xz = jnp.einsum('btd,ed->bte', x, W_in)
        xc, z = jnp.split(xz, 2, axis=-1)
        xp = jnp.pad(xc, ((0, 0), (1, 1), (0, 0)))
        xconv = xp[:, :-2] * conv_w[:, 0] + xp[:, 1:-1] * conv_w[:, 1] + xp[:, 2:] * conv_w[:, 2]
        xs = jax.nn.silu(xconv)
        x_dbl = jnp.einsum('btd,ed->bte', xs, W_x)
        dt_param = x_dbl[..., :R]
        Bp = x_dbl[..., R:R + N]
        Cp = x_dbl[..., R + N:]
        dt = jax.nn.softplus(dt_param @ W_dt.T + b_dt) + 1e-05
        A_disc = jnp.exp(-jnp.exp(A_log)[None, None] * dt[..., None])
        Bx = Bp[:, :, None, :] * dt[..., None] * xs[..., None]
        C = Cp @ W_C.T

        def step(s, inp):
            A_t, Bx_t = inp
            s = A_t * s + Bx_t
            return (s, s.sum(-1))
        s0 = jnp.zeros((x.shape[0], D, N), x.dtype)
        _, ssum = jax.lax.scan(step, s0, (A_disc.transpose(1, 0, 2, 3), Bx.transpose(1, 0, 2, 3)))
        ssum = ssum.transpose(1, 0, 2)
        y = C * ssum + D_param * xs
        return jnp.einsum('btd,ed->bte', y, W_out) * jax.nn.silu(z)

    def _L0_ffn_ref(x, gate_w, w1, b1, w2, b2, sw1, sb1, sw2, sb2):
        import jax, jax.numpy as jnp
        import numpy as np
        D_MODEL = 128
        HIDDEN = 512
        N_ROUTING = 2
        B, S, D = x.shape
        xf = x.reshape(-1, D)
        gate_scores = xf @ gate_w.T
        gate_probs = jax.nn.softmax(gate_scores, axis=-1)
        top1 = jnp.argmax(gate_probs, axis=-1)
        one_hot = jax.nn.one_hot(top1, N_ROUTING, dtype=xf.dtype)
        masked = xf[None, :, :] * one_hot.T[:, :, None]
        h = jax.nn.relu(jnp.einsum('end,edh->enh', masked, w1) + b1[:, None, :])
        expert_out = jnp.einsum('enh,ehd->end', h, w2) + b2[:, None, :]
        routing_output = expert_out.sum(axis=0)
        shared = jax.nn.relu(xf @ sw1 + sb1) @ sw2 + sb2
        return (routing_output + shared).reshape(B, S, D)
    x = L0_attn_x
    mod = (_silu(L0_c) @ L0_wmod).reshape(L0_c.shape[0], 6, 1, -1)
    sa, ca, ga, sb, cb, gb = (mod[:, 0], mod[:, 1], mod[:, 2], mod[:, 3], mod[:, 4], mod[:, 5])
    ga = (2 * (ga >= 0) - 1) * jnp.maximum(jnp.abs(ga), 0.25)
    gb = (2 * (gb >= 0) - 1) * jnp.maximum(jnp.abs(gb), 0.25)
    h = _layernorm(x, axis=-1) * (1 + ca) + sa
    x = x + ga * _L0_attn_ref(h, L0_attn_W_in, L0_attn_conv_w, L0_attn_W_x, L0_attn_W_dt, L0_attn_b_dt, L0_attn_A_log, L0_attn_D_param, L0_attn_W_C, L0_attn_W_out)
    h = _layernorm(x, axis=-1) * (1 + cb) + sb
    x = x + gb * _L0_ffn_ref(h, L0_ffn_gate_w, L0_ffn_w1, L0_ffn_b1, L0_ffn_w2, L0_ffn_b2, L0_ffn_sw1, L0_ffn_sb1, L0_ffn_sw2, L0_ffn_sb2)
    return x

_drawn_inputs = setup_inputs


def setup_inputs(seed=0):
    import zlib

    import numpy as np

    out = dict(_drawn_inputs(seed))
    spreads = {'L0_attn_b_dt': (1.0, 0.2), 'L0_attn_A_log': (-2.0, 0.6), 'L0_attn_D_param': (1.0, 0.6)}
    factors = {'L0_attn_W_in': 8.0,
     'L0_attn_conv_w': 8.0,
     'L0_attn_W_x': 8.0,
     'L0_attn_W_C': 8.0,
     'L0_attn_W_out': 8.0,
     'L0_ffn_gate_w': 4.449,
     'L0_ffn_w1': 3.794,
     'L0_ffn_b1': 8.0,
     'L0_ffn_w2': 3.107,
     'L0_ffn_b2': 7.428,
     'L0_ffn_sw1': 3.837,
     'L0_ffn_sb1': 8.0,
     'L0_ffn_sw2': 3.105,
     'L0_ffn_sb2': 8.0}
    for name, (base, spread) in spreads.items():
        noise = np.random.default_rng([zlib.crc32(name.encode()), seed]).standard_normal(out[name].shape)
        drawn = base * np.exp(spread * noise) if base else spread * noise
        out[name] = jnp.asarray(drawn.astype(out[name].dtype))
    for name, factor in factors.items():
        out[name] = (out[name] * factor).astype(out[name].dtype)
    return out
```

```python
from contextlib import ExitStack

import numpy as np

import concourse.bass as bass
from concourse import mybir

FP32 = mybir.dt.float32
FP32R = mybir.dt.float32r
BF16 = mybir.dt.bfloat16
ALU = mybir.AluOpType
ACT = mybir.ActivationFunctionType
AX = mybir.AxisListType.X

BATCH, T, D = 8, 512, 128
STATES, RANK, HIDDEN, EXPERTS = 16, 64, 512, 2
NETS = EXPERTS + 1
CHUNKS = T // 128
HCH = HIDDEN // 128
TILES = NETS * HCH
PER_UNIT = 2
UNITS = STATES // PER_UNIT
ADDS = UNITS - 1
HALF = 32
LN_EPS, DT_EPS, GATE_FLOOR = 1e-5, 1e-5, 0.25
RING = 4
G_RING = 3

COLS = {}
_at = 0
for _name, _n in (("conv", 3), ("b_dt", 1), ("a_log", STATES), ("d", 1), ("b1", TILES), ("b2", NETS),
                  ("c", BATCH), ("gate", EXPERTS)):
    COLS[_name] = (_at, _at + _n)
    _at += _n
N_COLS = _at

SLOT_TILES = [list(range(TILES * k // UNITS, TILES * (k + 1) // UNITS)) for k in range(UNITS)]

MISC_ORDER = [("b", 1), ("gate", -2), ("c", -1), ("o", -1), ("mask", -2), ("dt", 1), ("x2t", -1), ("xn2t", -1)]


def adaln_kernel(nc, x, xT, cols, wsq, wmod, wlow, w1, w2, sel, ident, outT):
    ctx = ExitStack()
    with ctx:
        def sb(name, shape, dt=FP32):
            return ctx.enter_context(nc.sbuf_tensor(name, shape, dt))

        def sem(name):
            return ctx.enter_context(nc.semaphore(name))

        cols_sb = sb("cols_sb", [128, N_COLS])
        wsq_sb = sb("wsq_sb", [128, 4 * D])
        wmod_sb = sb("wmod_sb", [128, 6 * D])
        wlow_sb = sb("wlow_sb", [RANK, 4 * D])
        w1_sb = sb("w1_sb", [128, NETS, HIDDEN])
        w2_sb = sb("w2_sb", [128, NETS, HCH, D])
        sel_in = sb("sel_in", [128, STATES])
        ident_sb = sb("ident_sb", [128, 128])
        ident_bf = sb("ident_bf", [128, 128], BF16)
        sel_sb = sb("sel_sb", [128, STATES, 128], FP32R)
        m_dt = sb("m_dt", [128, D])
        m_c = sb("m_c", [128, D])
        a_pos = sb("a_pos", [128, STATES])
        a_neg = sb("a_neg", [128, STATES])
        b2_sum = sb("b2_sum", [128, 1])
        b2_gb = sb("b2_gb", [128, BATCH])
        c_silu = sb("c_silu", [128, BATCH])
        mod = sb("mod", [128, 6, BATCH])
        g_sign = sb("g_sign", [128, BATCH])
        g_size = sb("g_size", [128, BATCH])
        ones_col = sb("ones_col", [128, 1])
        half_neg = sb("half_neg", [128, CHUNKS])
        eps_row = sb("eps_row", [128, CHUNKS])

        def col(name, i=0, n=1):
            return cols_sb[:, COLS[name][0] + i:COLS[name][0] + i + n]

        w_xc, w_z = wsq_sb[:, 0:D], wsq_sb[:, D:2 * D]
        w_out = wsq_sb[:, 2 * D:3 * D]
        w_b = wsq_sb[:, 3 * D:4 * D]

        x_res = sb("x_res", [128, BATCH * T])
        xs_all = sb("xs_all", [128, BATCH * T])
        zs_all = sb("zs_all", [128, BATCH * T])
        dt_two = sb("dt_two", [128, 2, T])
        u_two = sb("u_two", [128, 2, T])
        b_two = sb("b_two", [128, 2, T], FP32R)

        x_tok = sb("x_tok", [128, 2, CHUNKS, D])
        a_stats = sb("a_stats", [128, 2, CHUNKS, 6])
        a_mv = sb("a_mv", [128, 2, CHUNKS, 2])
        a_var = sb("a_var", [128, 2, CHUNKS])
        a_rstd = sb("a_rstd", [128, 2, CHUNKS])
        x_norm = sb("x_norm", [128, 2, CHUNKS, D])
        h1 = sb("h1", [128, 2, T])
        conv = sb("conv", [128, 2, T])

        dt_log, dt_pos = conv[:, 0], conv[:, 1]
        y_sb, attn = h1[:, 0], h1[:, 1]
        x2_norm = x_norm[:, 0]
        a_ring = sb("a_ring", [128, RING, PER_UNIT, T])
        s_ring = sb("s_ring", [128, RING, PER_UNIT, T])
        s_acc = sb("s_acc", [128, PER_UNIT, T])
        s_sum = sb("s_sum", [128, T])
        dt_abs = sb("dt_abs", [128, T])
        x2 = sb("x2", [128, CHUNKS, 128])
        b_stats = sb("b_stats", [128, CHUNKS, 6])
        b_mv = sb("b_mv", [128, CHUNKS, 2])
        b_var = sb("b_var", [128, CHUNKS])
        b_rstd = sb("b_rstd", [128, CHUNKS])
        h2 = sb("h2", [128, NETS, T])
        g_max = sb("g_max", [128, CHUNKS])
        g_sub = sb("g_sub", [128, CHUNKS, EXPERTS])
        g_exp = sb("g_exp", [128, CHUNKS, EXPERTS])
        g_den = sb("g_den", [128, CHUNKS])
        g_inv = sb("g_inv", [128, CHUNKS])
        g_prob = sb("g_prob", [128, CHUNKS, EXPERTS])
        g_first = sb("g_first", [128, CHUNKS], BF16)
        g_ring = sb("g_ring", [128, G_RING, T])
        out_sb = sb("out_sb", [128, T])

        bank = ctx.enter_context(nc.psum_tensor("bank", [128, 8, 512], FP32))
        misc = bank[:, 7, :]
        net_out = bank[:, 6, :]

        ld_cols, ld_wsq, ld_wmod, ld_wlow = sem("ld_cols"), sem("ld_wsq"), sem("ld_wmod"), sem("ld_wlow")
        ld_w1, ld_w2, ld_sel, ld_ident, ld_xT = sem("ld_w1"), sem("ld_w2"), sem("ld_sel"), sem("ld_ident"), sem("ld_xT")
        ld_x = [sem("ld_x_even"), sem("ld_x_odd")]
        consts_set, sel_done, ident_done, cond_done = sem("consts_set"), sem("sel_done"), sem("ident_done"), sem("cond_done")
        mod_mm, low_mm, mod_done, low_done = sem("mod_mm"), sem("low_mm"), sem("mod_done"), sem("low_done")
        a_exp_done, a_done, mod_step = sem("a_exp_done"), sem("a_done"), sem("mod_step")
        a_stats_done, a_mv_done = sem("a_stats_done"), sem("a_mv_done")
        a_var_done, a_rstd_done = sem("a_var_done"), sem("a_rstd_done")
        a_norm_done, a_xt_done, a_h_done = sem("a_norm_done"), sem("a_xt_done"), sem("a_h_done")
        xc_mm, z_mm, conv_mid, conv_done = sem("xc_mm"), sem("z_mm"), sem("conv_mid"), sem("conv_done")
        zs_done, xs_done = sem("zs_done"), sem("xs_done")
        b_mm, b_hi, b_lo, dt_mm = sem("b_mm"), sem("b_hi"), sem("b_lo"), sem("dt_mm")
        dt_act, dt_relu, dt_done, u_done = sem("dt_act"), sem("dt_relu"), sem("dt_done"), sem("u_done")
        b_cast, decay_done, bu_done, scan_done = sem("b_cast"), sem("decay_done"), sem("bu_done"), sem("scan_done")
        units_added, sum_done = sem("units_added"), sem("sum_done")
        c_mm, cs_done, y_done, o_mm, attn_done, x2_done = (sem("c_mm"), sem("cs_done"), sem("y_done"), sem("o_mm"),
                                                           sem("attn_done"), sem("x2_done"))
        x2t_mm, b_stats_done, b_mv_done = sem("x2t_mm"), sem("b_stats_done"), sem("b_mv_done")
        b_var_done, b_rstd_done, b_norm_done = sem("b_var_done"), sem("b_rstd_done"), sem("b_norm_done")
        x2b_done, xn2t_mm, h2_done = sem("x2b_done"), sem("xn2t_mm"), sem("h2_done")
        gate_mm, gate_dve, gate_exp = sem("gate_mm"), sem("gate_dve"), sem("gate_exp")
        mask_mm, first_done, second_done = sem("mask_mm"), sem("first_done"), sem("second_done")
        hid_mm, hid_done, net_mm = sem("hid_mm"), sem("hid_done"), sem("net_mm")
        out_done, stored = sem("out_done"), sem("stored")

        MISC_FREED = {"b": [(b_lo, 1)], "gate": [(gate_dve, 6)], "c": [(cs_done, 1)], "o": [(attn_done, 1)],
                      "mask": [(first_done, 1)], "dt": [(dt_relu, 1), (dt_act, 3)], "x2t": [(b_norm_done, CHUNKS)],
                      "xn2t": [(h2_done, 1)]}
        GATE_SUB = 2

        def seq(tile, b):
            return tile[:, bass.ds(b * T, T)]

        def settled(eng):
            eng.wait_ge(consts_set, 4)

        def units_released(i, k):
            k -= RING
            if k < 0:
                i, k = i - 1, k + UNITS
            return ADDS * i + max(k, 1)

        def stages(i):
            if not isinstance(i, int):
                return dict.fromkeys(("prepare", "scan", "mix", "experts", "finish"), True)
            return {n: 0 <= i + o < BATCH for n, o in
                    (("prepare", 1), ("scan", 0), ("mix", -1), ("experts", -2), ("finish", -3))}

        FIRST_LOOPED, END_LOOPED = 3, BATCH - 1

        def run_steps(eng, step):
            for i in range(-1, FIRST_LOOPED):
                step(i, i % 2)
            with eng.Fori(0, (END_LOOPED - FIRST_LOOPED) // 2) as q:
                for half in range(2):
                    step(FIRST_LOOPED + half + 2 * q, (FIRST_LOOPED + half) % 2)
            for i in range(END_LOOPED, BATCH + 3):
                step(i, i % 2)

        block = ctx.enter_context(nc.Block())

        @block.sync
        def _(sp):
            x_v = x.rearrange("b (c p) d -> b p c d", p=128)
            sp.dma_start(x_tok[:, 0], x_v[0]).then_inc(ld_x[0], 16)
            sp.dma_start(ident_sb[:], ident).then_inc(ld_ident, 16)
            sp.dma_start(wsq_sb[:], wsq).then_inc(ld_wsq, 16)
            sp.dma_start(x_tok[:, 1], x_v[1]).then_inc(ld_x[1], 16)
            sp.dma_start(wlow_sb[:], wlow).then_inc(ld_wlow, 16)
            sp.dma_start(sel_in[:], sel).then_inc(ld_sel, 16)
            for b in range(2, BATCH):
                sp.wait_ge(a_norm_done, CHUNKS * (b - 1))
                sp.dma_start(x_tok[:, b % 2], x_v[b]).then_inc(ld_x[b % 2], 16)
                if b == 4:
                    sp.dma_start(x_res[:], xT).then_inc(ld_xT, 16)
                    sp.dma_start(w1_sb[:], w1).then_inc(ld_w1, 16)
                    sp.dma_start(w2_sb[:], w2).then_inc(ld_w2, 16)
            with sp.Fori(0, BATCH) as b:
                sp.wait_ge(out_done, b + 1)
                sp.dma_start(outT[:, bass.ds(b * T, T)], out_sb[:]).then_inc(stored, 16)
            sp.wait_ge(stored, 16 * BATCH)

        @block.tensor
        def _(pe):
            pe.wait_ge(ld_wmod, 16)
            pe.wait_ge(cond_done, 1)
            for m in range(6):
                last = nc.tensor.matmul(bank[:, 2, m * BATCH:(m + 1) * BATCH], wmod_sb[:, m * D:(m + 1) * D], c_silu[:],
                                        start=True, stop=True)
            last.then_inc(mod_mm, 1)

            def transposes(b, par):
                pe.wait_ge(a_norm_done, CHUNKS * b + CHUNKS)
                if not isinstance(b, int) or b >= 2:
                    pe.wait_ge(a_h_done, b - 1)
                for c in range(CHUNKS):
                    last = nc.tensor.transpose(bank[:, 4 + par, c * 128:(c + 1) * 128], x_norm[:, par, c], ident_sb[:])
                last.then_inc(a_xt_done, 1)

            def project(b, par):
                pe.wait_ge(a_h_done, b + 1)
                if not isinstance(b, int) or b >= 2:
                    pe.wait_ge(conv_done, 2 * b - 2)
                nc.tensor.matmul(bank[:, 6 + par], w_xc, h1[:, par], start=True, stop=True).then_inc(xc_mm, 1)
                if not isinstance(b, int) or b >= 2:
                    pe.wait_ge(zs_done, b - 1)
                nc.tensor.matmul(bank[:, par], w_z, h1[:, par], start=True, stop=True).then_inc(z_mm, 1)

            pe.wait_ge(ld_ident, 16)
            transposes(0, 0)
            pe.wait_ge(ld_wlow, 16)
            nc.tensor.matmul(bank[:, 3, 0:D], wlow_sb[:, 0:D], wlow_sb[:, D:2 * D], start=True, stop=True)
            nc.tensor.matmul(bank[:, 3, D:2 * D], wlow_sb[:, 2 * D:3 * D], wlow_sb[:, 3 * D:4 * D],
                             start=True, stop=True).then_inc(low_mm, 1)
            pe.wait_ge(ld_wsq, 16)
            transposes(1, 1)
            project(0, 0)
            with pe.Fori(0, BATCH // 2 - 1) as q:
                b = 2 * q + 1
                transposes(b + 1, 0)
                project(b, 1)
                transposes(b + 2, 1)
                project(b + 1, 0)
            project(BATCH - 1, 1)
            pe.wait_ge(conv_done, 2 * BATCH)
            pe.wait_ge(zs_done, BATCH)
            pe.wait_ge(low_done, 2)
            pe.wait_ge(mod_done, 1)
            pe.wait_ge(xs_done, BATCH)
            pe.wait_ge(sel_done, 1)
            pe.wait_ge(ident_done, 1)
            pe.wait_ge(ld_w1, 16)
            pe.wait_ge(ld_w2, 16)

            def misc_free(user, i):
                names = [n for n, _ in MISC_ORDER]
                at = names.index(user)
                if isinstance(i, int):
                    for n, (name, o) in enumerate(MISC_ORDER):
                        done = min(max(i + o + (n < at), 0), BATCH)
                        if done and name != user:
                            for s, per in MISC_FREED[name]:
                                pe.wait_ge(s, per * (done - 1) + (GATE_SUB if name == "gate" else per))
                else:
                    name, o = MISC_ORDER[at - 1]
                    b = i + o - (at == 0)
                    for s, per in MISC_FREED[name]:
                        pe.wait_ge(s, per * b + (GATE_SUB if name == "gate" else per))

            def step(i, par):
                on = stages(i)
                p, j, f = i + 1, i - 1, i - 2

                def hidden(t):
                    if t == HCH:
                        pe.wait_ge(first_done, f + 1)
                    if t == 2 * HCH:
                        pe.wait_ge(second_done, f + 1)
                    n = TILES * f + t - 1
                    if not isinstance(f, int) or n > 0:
                        pe.wait_ge(hid_done, n)
                    e, m = divmod(t, HCH)
                    nc.tensor.matmul(bank[:, 4 + t % 2], w1_sb[:, e, m * 128:(m + 1) * 128], h2[:, e],
                                     start=True, stop=True).then_inc(hid_mm, 1)

                def output(t):
                    e, m = divmod(t, HCH)
                    if t == 0 and (not isinstance(f, int) or f > 0):
                        pe.wait_ge(out_done, f)
                    pe.wait_ge(hid_done, TILES * f + t + 1)
                    nc.tensor.matmul(net_out, w2_sb[:, e, m], g_ring[:, t % G_RING],
                                     start=(t == 0), stop=(t == TILES - 1)).then_inc(net_mm, 1)

                def experts_tiles(k):
                    for t in SLOT_TILES[k]:
                        hidden(t)
                        if t:
                            output(t - 1)
                    if k == UNITS - 1:
                        output(TILES - 1)

                for k in range(UNITS):
                    if on["scan"]:
                        if k == 0:
                            pe.wait_ge(b_lo, i + 1)
                        n = UNITS * i + k - 1
                        if not isinstance(i, int) or n > 0:
                            pe.wait_ge(scan_done, n)
                        for s in range(PER_UNIT):
                            last = nc.tensor.matmul(bank[:, PER_UNIT * (k % 2) + s], sel_sb[:, PER_UNIT * k + s],
                                                    b_two[:, par], start=True, stop=True)
                        last.then_inc(b_cast, 1)
                    if k == 0 and on["prepare"]:
                        misc_free("b", i)
                        nc.tensor.matmul(misc, w_b, seq(xs_all, p), start=True, stop=True).then_inc(b_mm, 1)
                    if k == 0 and on["experts"]:
                        misc_free("gate", i)
                        pe.wait_ge(h2_done, f + 1)
                        for c in range(CHUNKS):
                            last = nc.tensor.matmul(misc[:, EXPERTS * c:EXPERTS * (c + 1)], h2[:, 0, c * 128:(c + 1) * 128],
                                                    col("gate", 0, EXPERTS), start=True, stop=True)
                        last.then_inc(gate_mm, 1)
                    if k == 1 and on["mix"]:
                        misc_free("c", i)
                        nc.tensor.matmul(misc, m_c[:], seq(xs_all, j), start=True, stop=True).then_inc(c_mm, 1)
                    if k == 2 and on["mix"]:
                        misc_free("o", i)
                        pe.wait_ge(y_done, j + 1)
                        nc.tensor.matmul(misc, w_out, y_sb, start=True, stop=True).then_inc(o_mm, 1)
                    if k == 4 and on["prepare"]:
                        misc_free("dt", i)
                        nc.tensor.matmul(misc, m_dt[:], seq(xs_all, p), start=True, stop=True).then_inc(dt_mm, 1)
                    if k == 5 and on["mix"]:
                        misc_free("x2t", i)
                        pe.wait_ge(x2_done, j + 1)
                        for c in range(CHUNKS):
                            last = nc.tensor.transpose(misc[:, c * 128:(c + 1) * 128], x2[:, c], ident_sb[:])
                        last.then_inc(x2t_mm, 1)
                    if on["experts"]:
                        experts_tiles(k)
                    if k == 2 and on["experts"]:
                        misc_free("mask", i)
                        pe.wait_ge(gate_dve, 6 * f + 6)
                        for c in range(CHUNKS):
                            last = nc.tensor.matmul(misc[:, c * 128:(c + 1) * 128],
                                                    g_first[:, c:c + 1].to_broadcast([128, 128]), ident_bf[:],
                                                    start=True, stop=True)
                        last.then_inc(mask_mm, 1)
                if on["mix"]:
                    misc_free("xn2t", i)
                    pe.wait_ge(b_norm_done, CHUNKS * j + CHUNKS)
                    for c in range(CHUNKS):
                        last = nc.tensor.transpose(misc[:, c * 128:(c + 1) * 128], x2_norm[:, c], ident_sb[:])
                    last.then_inc(xn2t_mm, 1)

            run_steps(pe, step)

        @block.scalar
        def _(act):
            act.dma_start(cols_sb[:], cols).then_inc(ld_cols, 16)
            act.dma_start(wmod_sb[:], wmod).then_inc(ld_wmod, 16)
            act.wait_ge(ld_cols, 16)
            nc.scalar.activation(c_silu[:], col("c", 0, BATCH), ACT.Silu).then_inc(cond_done, 1)

            def modulate(b, par):
                act.wait_ge(a_xt_done, b + 1)
                if not isinstance(b, int) or b >= 2:
                    act.wait_ge(z_mm, b - 1)
                settled(act)
                nc.scalar.activation(h1[:, par], bank[:, 4 + par], ACT.Identity, bias=mod[:, 0, bass.ds(b, 1)],
                                     scale=mod[:, 1, bass.ds(b, 1)]).then_inc(a_h_done, 1)

            def middle_tap_and_z(b, par):
                act.wait_ge(xc_mm, b + 1)
                if not isinstance(b, int) or b >= 2:
                    act.wait_ge(xs_done, b - 1)
                nc.scalar.activation(conv[:, par], bank[:, 6 + par], ACT.Copy, scale=col("conv", 1)).then_inc(conv_mid, 1)
                act.wait_ge(z_mm, b + 1)
                settled(act)
                nc.scalar.activation(seq(zs_all, b), bank[:, par], ACT.Silu).then_inc(zs_done, 1)

            def silu_conv(b, par):
                act.wait_ge(conv_done, 2 * b + 2)
                settled(act)
                nc.scalar.activation(seq(xs_all, b), conv[:, par], ACT.Silu).then_inc(xs_done, 1)

            act.wait_ge(mod_done, 1)
            modulate(0, 0)
            middle_tap_and_z(0, 0)
            modulate(1, 1)
            with act.Fori(0, BATCH // 2 - 1) as q:
                b = 2 * q + 1
                silu_conv(b - 1, 0)
                middle_tap_and_z(b, 1)
                modulate(b + 1, 0)
                silu_conv(b, 1)
                middle_tap_and_z(b + 1, 0)
                modulate(b + 2, 1)
            silu_conv(BATCH - 2, 0)
            middle_tap_and_z(BATCH - 1, 1)
            silu_conv(BATCH - 1, 1)
            nc.scalar.activation(a_pos[:], col("a_log", 0, STATES), ACT.Exp).then_inc(a_exp_done, 1)
            act.wait_ge(a_exp_done, 1)
            nc.scalar.activation(a_neg[:], a_pos[:], ACT.Copy, scale=-1.0).then_inc(a_done, 1)
            act.wait_ge(a_done, 1)
            act.wait_ge(consts_set, 4)

            def step(i, par):
                on = stages(i)
                p, j, f = i + 1, i - 1, i - 2
                for k in range(UNITS):
                    if on["scan"]:
                        if k == 0:
                            act.wait_ge(dt_done, i + 1)
                        n = UNITS * i + k - RING + 1
                        if not isinstance(i, int) or n > 0:
                            act.wait_ge(scan_done, n)
                        for s in range(PER_UNIT):
                            n = PER_UNIT * k + s
                            last = nc.scalar.activation(
                                a_ring[:, k % RING, s, 1:T], dt_two[:, par, 1:T], ACT.Exp,
                                scale=a_neg[:, n:n + 1])
                        last.then_inc(decay_done, 1)
                    if k == 0 and on["prepare"]:
                        act.wait_ge(b_mm, p + 1)
                        settled(act)
                        nc.scalar.activation(b_two[:, 1 - par], misc, ACT.Copy).then_inc(b_hi, 1)
                    if k == 1 and on["experts"]:
                        act.wait_ge(gate_dve, 6 * f + 2)
                        nc.scalar.activation(g_exp[:], g_sub[:], ACT.Exp).then_inc(gate_exp, 1)
                    if on["experts"]:
                        for t in SLOT_TILES[k]:
                            act.wait_ge(hid_mm, TILES * f + t + 1)
                            n = TILES * f + t - G_RING + 1
                            if not isinstance(f, int) or n > 0:
                                act.wait_ge(net_mm, n)
                            nc.scalar.activation(g_ring[:, t % G_RING], bank[:, 4 + t % 2], ACT.Relu,
                                                 bias=col("b1", t)).then_inc(hid_done, 1)
                    if k == 4 and on["prepare"]:
                        act.wait_ge(dt_mm, p + 1)
                        if not isinstance(p, int) or p > 0:
                            act.wait_ge(dt_done, p)
                        nc.scalar.activation(dt_abs[:], misc, ACT.Abs, bias=col("b_dt")).then_inc(dt_act, 1)
                        act.wait_ge(dt_act, 3 * p + 1)
                        nc.scalar.activation(dt_abs[:], dt_abs[:], ACT.Exp, scale=-1.0).then_inc(dt_act, 1)
                        act.wait_ge(dt_act, 3 * p + 2)
                        nc.scalar.activation(dt_log, dt_abs[:], ACT.Ln, bias=ones_col[:]).then_inc(dt_act, 1)
                    if k == 5 and on["mix"]:
                        act.wait_ge(x2_done, j + 1)
                        settled(act)
                        nc.scalar.activation(seq(x_res, j), x2[:].rearrange("p c t -> p (c t)"), ACT.Identity,
                                             bias=b2_gb[:, bass.ds(j, 1)]).then_inc(x2b_done, 1)
                if on["mix"]:
                    act.wait_ge(xn2t_mm, j + 1)
                    if not isinstance(j, int) or j > 0:
                        act.wait_ge(second_done, j)
                        act.wait_ge(hid_mm, TILES * (j - 1) + HCH)
                    settled(act)
                    nc.scalar.activation(h2[:, 0], misc, ACT.Identity, bias=mod[:, 3, bass.ds(j, 1)],
                                         scale=mod[:, 4, bass.ds(j, 1)]).then_inc(h2_done, 1)

            run_steps(act, step)

        @block.vector
        def _(dve):
            nc.vector.memset(ones_col[:], 1.0).then_inc(consts_set, 1)
            nc.vector.memset(half_neg[:], -0.5).then_inc(consts_set, 1)
            nc.vector.memset(a_ring[:, :, :, 0:1], 0.0).then_inc(consts_set, 1)
            nc.vector.memset(eps_row[:], LN_EPS).then_inc(consts_set, 1)

            def statistics(b, par):
                for c in range(CHUNKS):
                    nc.vector.bn_stats(a_stats[:, par, c], x_tok[:, par, c]).then_inc(a_stats_done, 1)

            def aggregate(b, par):
                for c in range(CHUNKS):
                    nc.vector.bn_aggr(a_mv[:, par, c], a_stats[:, par, c]).then_inc(a_mv_done, 1)

            def normalise(b, par):
                dve.wait_ge(a_rstd_done, b + 1)
                if not isinstance(b, int) or b >= 2:
                    dve.wait_ge(a_xt_done, b - 1)
                for c in range(CHUNKS):
                    nc.vector.tensor_scalar(x_norm[:, par, c], x_tok[:, par, c], a_mv[:, par, c, 0:1],
                                            a_rstd[:, par, c:c + 1], ALU.subtract, ALU.mult).then_inc(a_norm_done, 1)

            def convolve(b, par):
                xc = bank[:, 6 + par]
                if not isinstance(b, int):
                    dve.wait_ge(a_stats_done, CHUNKS * b + 3 * CHUNKS)
                dve.wait_ge(conv_mid, b + 1)
                nc.vector.scalar_tensor_tensor(conv[:, par, 1:T], xc[:, 0:T - 1], col("conv", 0), conv[:, par, 1:T],
                                               ALU.mult, ALU.add).then_inc(conv_done, 1)
                dve.wait_ge(conv_done, 2 * b + 1)
                nc.vector.scalar_tensor_tensor(conv[:, par, 0:T - 1], xc[:, 1:T], col("conv", 2), conv[:, par, 0:T - 1],
                                               ALU.mult, ALU.add).then_inc(conv_done, 1)

            dve.wait_ge(ld_x[0], 16)
            statistics(0, 0)
            dve.wait_ge(a_stats_done, CHUNKS)
            aggregate(0, 0)
            dve.wait_ge(mod_mm, 1)
            mps = bank[:, 2, 0:6 * BATCH].rearrange("p (m b) -> p m b", b=BATCH)
            nc.vector.tensor_copy(mod[:], mps).then_inc(mod_step, 1)
            dve.wait_ge(mod_step, 1)
            step_n = 1
            for m in (1, 4):
                nc.vector.tensor_scalar(mod[:, m], mod[:, m], 1.0, None, ALU.add).then_inc(mod_step, 1)
                step_n += 1
            for m in (2, 5):
                dve.wait_ge(mod_step, step_n)
                nc.vector.tensor_scalar(g_sign[:], mod[:, m], 0.0, 2.0, ALU.is_ge, ALU.mult).then_inc(mod_step, 1)
                nc.vector.tensor_scalar(g_size[:], mod[:, m], -1.0, GATE_FLOOR, ALU.mult, ALU.max).then_inc(mod_step, 1)
                step_n += 2
                dve.wait_ge(mod_step, step_n)
                nc.vector.tensor_tensor(g_size[:], mod[:, m], g_size[:], ALU.max).then_inc(mod_step, 1)
                step_n += 1
                dve.wait_ge(mod_step, step_n)
                nc.vector.scalar_tensor_tensor(mod[:, m], g_sign[:], -1.0, g_size[:], ALU.add, ALU.mult).then_inc(mod_step, 1)
                step_n += 1
            dve.wait_ge(mod_step, step_n)
            nc.vector.tensor_tensor(b2_sum[:], col("b2", 0), col("b2", 1), ALU.add).then_inc(mod_step, 1)
            dve.wait_ge(mod_step, step_n + 1)
            nc.vector.tensor_tensor(b2_sum[:], b2_sum[:], col("b2", 2), ALU.add).then_inc(mod_step, 1)
            dve.wait_ge(mod_step, step_n + 2)
            nc.vector.tensor_scalar(b2_gb[:], mod[:, 5], b2_sum[:], None, ALU.mult).then_inc(mod_done, 1)
            normalise(0, 0)
            dve.wait_ge(ld_x[1], 16)
            statistics(1, 1)
            dve.wait_ge(a_stats_done, 2 * CHUNKS)
            aggregate(1, 1)
            dve.wait_ge(low_mm, 1)
            nc.vector.tensor_copy(m_dt[:], bank[:, 3, 0:D]).then_inc(low_done, 1)
            nc.vector.tensor_copy(m_c[:], bank[:, 3, D:2 * D]).then_inc(low_done, 1)
            dve.wait_ge(ld_ident, 16)
            nc.vector.tensor_copy(ident_bf[:], ident_sb[:]).then_inc(ident_done, 1)
            normalise(1, 1)
            with dve.Fori(1, BATCH // 2) as q:
                dve.wait_ge(ld_x[0], 16 * q + 16)
                statistics(2 * q, 0)
                convolve(2 * q - 2, 0)
                aggregate(2 * q, 0)
                normalise(2 * q, 0)
                dve.wait_ge(ld_x[1], 16 * q + 16)
                statistics(2 * q + 1, 1)
                convolve(2 * q - 1, 1)
                aggregate(2 * q + 1, 1)
                normalise(2 * q + 1, 1)
            convolve(BATCH - 2, 0)
            convolve(BATCH - 1, 1)

            def step(i, par):
                on = stages(i)
                p, j, f, w = i + 1, i - 1, i - 2, i - 3
                for k in range(UNITS):
                    pair = bank[:, PER_UNIT * (k % 2):PER_UNIT * (k % 2) + PER_UNIT]
                    if on["scan"]:
                        if k == 0:
                            dve.wait_ge(u_done, i + 1)
                        dve.wait_ge(b_cast, UNITS * i + k + 1)
                        u_rep = u_two[:, par].unsqueeze(1).to_broadcast([128, PER_UNIT, T])
                        nc.vector.tensor_tensor(pair, pair, u_rep, ALU.mult).then_inc(bu_done, 1)
                    if k == 0 and on["finish"]:
                        dve.wait_ge(net_mm, TILES * w + TILES)
                        dve.wait_ge(x2b_done, w + 1)
                        if not isinstance(w, int) or w > 0:
                            dve.wait_ge(stored, 16 * w)
                        nc.vector.scalar_tensor_tensor(out_sb[:], net_out, mod[:, 5, bass.ds(w, 1)], seq(x_res, w),
                                                       ALU.mult, ALU.add).then_inc(out_done, 1)
                    if k == 0 and on["prepare"]:
                        dve.wait_ge(b_hi, p + 1)
                        low = b_two[HALF:2 * HALF, 1 - par]
                        nc.vector.tensor_tensor(low, misc[HALF:2 * HALF], low, ALU.subtract).then_inc(b_lo, 1)
                    if k == 1 and on["experts"]:
                        scores = misc[:, 0:EXPERTS * CHUNKS].rearrange("p (c e) -> p c e", e=EXPERTS)
                        dve.wait_ge(gate_mm, f + 1)
                        nc.vector.tensor_reduce(g_max[:], scores, AX, ALU.max).then_inc(gate_dve, 1)
                        dve.wait_ge(gate_dve, 6 * f + 1)
                        nc.vector.tensor_tensor(g_sub[:], scores, g_max[:].unsqueeze(2).to_broadcast([128, CHUNKS, EXPERTS]),
                                                ALU.subtract).then_inc(gate_dve, 1)
                    if k == 1 and on["mix"]:
                        dve.wait_ge(c_mm, j + 1)
                        dve.wait_ge(sum_done, j + 1)
                        nc.vector.tensor_tensor(y_sb, misc, s_sum[:], ALU.mult).then_inc(cs_done, 1)
                        dve.wait_ge(cs_done, j + 1)
                        nc.vector.scalar_tensor_tensor(y_sb, seq(xs_all, j), col("d"), y_sb,
                                                       ALU.mult, ALU.add).then_inc(y_done, 1)
                    if k == 2 and on["mix"]:
                        dve.wait_ge(o_mm, j + 1)
                        nc.vector.scalar_tensor_tensor(attn, misc, mod[:, 2, bass.ds(j, 1)], seq(zs_all, j),
                                                       ALU.mult, ALU.mult).then_inc(attn_done, 1)
                    if k == 3 and on["experts"]:
                        dve.wait_ge(mask_mm, f + 1)
                        nc.vector.tensor_tensor(h2[:, 1], misc, h2[:, 0], ALU.mult).then_inc(first_done, 1)
                    if k == 5 and on["prepare"]:
                        dve.wait_ge(dt_act, 3 * p + 1)
                        nc.vector.tensor_scalar(dt_pos, misc, col("b_dt"), 0.0, ALU.add, ALU.max).then_inc(dt_relu, 1)
                        dve.wait_ge(dt_relu, p + 1)
                        dve.wait_ge(dt_act, 3 * p + 3)
                        nc.vector.scalar_tensor_tensor(dt_two[:, 1 - par], dt_log, DT_EPS, dt_pos,
                                                       ALU.add, ALU.add).then_inc(dt_done, 1)
                    if k == 6 and on["mix"]:
                        dve.wait_ge(x2t_mm, j + 1)
                        for c in range(CHUNKS):
                            nc.vector.bn_stats(b_stats[:, c], misc[:, c * 128:(c + 1) * 128]).then_inc(b_stats_done, 1)
                        dve.wait_ge(b_stats_done, CHUNKS * j + CHUNKS)
                    if k == 7 and on["mix"]:
                        dve.wait_ge(b_rstd_done, j + 1)
                        for c in range(CHUNKS):
                            nc.vector.tensor_scalar(x2_norm[:, c], misc[:, c * 128:(c + 1) * 128], b_mv[:, c, 0:1],
                                                    b_rstd[:, c:c + 1], ALU.subtract, ALU.mult).then_inc(b_norm_done, 1)
                    if on["scan"]:
                        dve.wait_ge(bu_done, UNITS * i + k + 1)
                        dve.wait_ge(decay_done, UNITS * i + k + 1)
                        n = units_released(i, k)
                        if not isinstance(i, int) or UNITS * i + k >= RING:
                            dve.wait_ge(units_added, n)
                        nc.vector.tensor_tensor_scan(
                            s_ring[:, k % RING].rearrange("p s t -> p (s t)"),
                            a_ring[:, k % RING].rearrange("p s t -> p (s t)"),
                            pair.rearrange("p s t -> p (s t)"), 0.0, ALU.mult, ALU.add).then_inc(scan_done, 1)
                    if k == 6 and on["mix"]:
                        for c in range(CHUNKS):
                            nc.vector.bn_aggr(b_mv[:, c], b_stats[:, c]).then_inc(b_mv_done, 1)
                    if k == 1 and on["experts"]:
                        dve.wait_ge(gate_exp, f + 1)
                        nc.vector.tensor_reduce(g_den[:], g_exp[:], AX, ALU.add).then_inc(gate_dve, 1)
                        dve.wait_ge(gate_dve, 6 * f + 3)
                        nc.vector.reciprocal(g_inv[:], g_den[:]).then_inc(gate_dve, 1)
                        dve.wait_ge(gate_dve, 6 * f + 4)
                        nc.vector.tensor_tensor(g_prob[:], g_exp[:], g_inv[:].unsqueeze(2).to_broadcast([128, CHUNKS, EXPERTS]),
                                                ALU.mult).then_inc(gate_dve, 1)
                        dve.wait_ge(gate_dve, 6 * f + 5)
                        nc.vector.tensor_tensor(g_first[:], g_prob[:, :, 0], g_prob[:, :, 1], ALU.is_ge).then_inc(gate_dve, 1)

            run_steps(dve, step)

        @block.gpsimd
        def _(pool):
            pool.wait_ge(consts_set, 4)

            def a_rstd_of(b, par):
                pool.wait_ge(a_mv_done, CHUNKS * b + CHUNKS)
                nc.gpsimd.tensor_tensor(a_var[:, par], a_mv[:, par, :, 1], eps_row[:], ALU.add).then_inc(a_var_done, 1)
                pool.wait_ge(a_var_done, b + 1)
                nc.gpsimd.tensor_tensor(a_rstd[:, par], a_var[:, par], half_neg[:], ALU.pow).then_inc(a_rstd_done, 1)

            a_rstd_of(0, 0)
            a_rstd_of(1, 1)
            pool.wait_ge(ld_sel, 16)
            nc.gpsimd.tensor_copy(sel_sb[:], sel_in[:].unsqueeze(2).to_broadcast([128, STATES, 128])).then_inc(sel_done, 1)
            with pool.Fori(1, BATCH // 2) as q:
                a_rstd_of(2 * q, 0)
                a_rstd_of(2 * q + 1, 1)
            pool.wait_ge(xs_done, BATCH)
            pool.wait_ge(ld_xT, 16)

            def step(i, par):
                on = stages(i)
                p, j, f = i + 1, i - 1, i - 2
                for k in range(UNITS):
                    if on["scan"] and k:
                        pool.wait_ge(scan_done, UNITS * i + k + 1)
                        n = ADDS * i + k - 1
                        if not isinstance(i, int) or n > 0:
                            pool.wait_ge(units_added, n)
                        if k == 1 and (not isinstance(i, int) or i > 0):
                            pool.wait_ge(sum_done, i)
                        into = s_ring[:, 0] if k == 1 else s_acc[:]
                        nc.gpsimd.tensor_tensor(s_acc[:], into, s_ring[:, k % RING], ALU.add).then_inc(units_added, 1)
                    if k == 2 and on["mix"]:
                        pool.wait_ge(attn_done, j + 1)
                        if not isinstance(j, int) or j > 0:
                            pool.wait_ge(x2b_done, j)
                        nc.gpsimd.tensor_tensor(x2[:].rearrange("p c t -> p (c t)"), attn, seq(x_res, j),
                                                ALU.add).then_inc(x2_done, 1)
                    if k == 3 and on["experts"]:
                        pool.wait_ge(first_done, f + 1)
                        nc.gpsimd.tensor_tensor(h2[:, 2], h2[:, 0], h2[:, 1], ALU.subtract).then_inc(second_done, 1)
                    if k == 5 and on["prepare"]:
                        pool.wait_ge(dt_done, p + 1)
                        nc.gpsimd.tensor_tensor(u_two[:, 1 - par], dt_two[:, 1 - par], seq(xs_all, p), ALU.mult).then_inc(u_done, 1)
                    if k == 6 and on["mix"]:
                        pool.wait_ge(b_mv_done, CHUNKS * j + CHUNKS)
                        nc.gpsimd.tensor_tensor(b_var[:], b_mv[:, :, 1], eps_row[:], ALU.add).then_inc(b_var_done, 1)
                        pool.wait_ge(b_var_done, j + 1)
                        nc.gpsimd.tensor_tensor(b_rstd[:], b_var[:], half_neg[:], ALU.pow).then_inc(b_rstd_done, 1)
                if on["scan"]:
                    pool.wait_ge(units_added, ADDS * i + ADDS)
                    if not isinstance(i, int) or i > 0:
                        pool.wait_ge(cs_done, i)
                    nc.gpsimd.tensor_tensor(s_sum[:], s_acc[:, 0], s_acc[:, 1], ALU.add).then_inc(sum_done, 1)

            run_steps(pool, step)


def kernel(**inputs):
    import concourse.bacc as bacc
    from concourse.bass_utils import run_bass_kernel_spmd

    g = {k: np.asarray(v) for k, v in inputs.items()}

    def put(a):
        return np.ascontiguousarray(a)

    x = g["L0_attn_x"]
    w_x = g["L0_attn_W_x"]
    zeros = np.zeros((D, HALF - STATES), np.float32)
    b_rows = w_x[RANK:RANK + STATES].T
    w_c_pad = np.zeros((RANK, 2 * D), np.float32)
    w_c_pad[:STATES, :D] = w_x[RANK + STATES:]
    w_c_pad[:STATES, D:] = g["L0_attn_W_C"].T
    w1 = np.stack([g["L0_ffn_sw1"], *g["L0_ffn_w1"]], 1)
    w2 = np.stack([g["L0_ffn_sw2"], *g["L0_ffn_w2"]], 0)
    b1 = np.stack([g["L0_ffn_sb1"], *g["L0_ffn_b1"]], 0)
    b2 = np.stack([g["L0_ffn_sb2"], *g["L0_ffn_b2"]], 0)
    sel = np.zeros((128, STATES), np.float32)
    for n in range(STATES):
        sel[n, n] = sel[HALF + n, n] = 1.0
    arrays = {
        "x": x,
        "xT": x.reshape(BATCH * T, D).T,
        "cols": np.concatenate([g["L0_attn_conv_w"], g["L0_attn_b_dt"][:, None], g["L0_attn_A_log"],
                                g["L0_attn_D_param"][:, None], b1.reshape(TILES, 128).T, b2.T, g["L0_c"].T,
                                g["L0_ffn_gate_w"].T], 1),
        "wsq": np.concatenate([g["L0_attn_W_in"].T, g["L0_attn_W_out"].T, b_rows, zeros, b_rows, zeros,
                               np.zeros((D, 128 - 2 * HALF), np.float32)], 1),
        "wmod": g["L0_wmod"],
        "wlow": np.concatenate([w_x[:RANK], g["L0_attn_W_dt"].T, w_c_pad], 1),
        "w1": w1,
        "w2": w2.reshape(NETS, HCH, 128, D).transpose(2, 0, 1, 3),
        "sel": sel,
        "ident": np.eye(128, dtype=np.float32),
    }
    nc = bacc.Bacc("TRN2", target_bir_lowering=False, num_devices=1)
    arrays = {f"in_{k}": put(v) for k, v in arrays.items()}
    aps = [nc.dram_tensor(k, v.shape, mybir.dt.from_np(v.dtype), kind="ExternalInput").ap() for k, v in arrays.items()]
    outT = nc.dram_tensor("outT", (D, BATCH * T), FP32, kind="ExternalOutput").ap()
    adaln_kernel(nc, *aps, outT)
    r = run_bass_kernel_spmd(nc, [arrays], core_ids=[0])
    return put(r.results[0]["outT"].reshape(D, BATCH, T).transpose(1, 2, 0))
```

```python
from contextlib import ExitStack

import numpy as np

import concourse.bass as bass
from concourse import mybir

FP32 = mybir.dt.float32
FP32R = mybir.dt.float32r
BF16 = mybir.dt.bfloat16
ALU = mybir.AluOpType
ACT = mybir.ActivationFunctionType
AX = mybir.AxisListType.X

BATCH, T, D = 8, 512, 128
STATES, RANK, HIDDEN, EXPERTS = 16, 64, 512, 2
NETS = EXPERTS + 1
CHUNKS = T // 128
HCH = HIDDEN // 128
TILES = NETS * HCH
PER_UNIT = 2
UNITS = STATES // PER_UNIT
ADDS = UNITS - 1
HALF = 32
LN_EPS, DT_EPS, GATE_FLOOR = 1e-5, 1e-5, 0.25
RING = 4
G_RING = 3

COLS = {}
_at = 0
for _name, _n in (("conv", 3), ("b_dt", 1), ("a_log", STATES), ("d", 1), ("b1", TILES), ("b2", NETS),
                  ("c", BATCH), ("gate", EXPERTS)):
    COLS[_name] = (_at, _at + _n)
    _at += _n
N_COLS = _at

SLOT_TILES = [list(range(TILES * k // UNITS, TILES * (k + 1) // UNITS)) for k in range(UNITS)]

MISC_ORDER = [("mask", -2), ("c", -1), ("o", -1), ("b", 1), ("x2t", -1), ("dt", 1), ("xn2t", -1), ("gate", -1)]


def adaln_kernel(nc, x, xT, cols, wsq, wmod, wlow, w1, w2, sel, ident, outT):
    ctx = ExitStack()
    with ctx:
        def sb(name, shape, dt=FP32):
            return ctx.enter_context(nc.sbuf_tensor(name, shape, dt))

        def sem(name):
            return ctx.enter_context(nc.semaphore(name))

        cols_sb = sb("cols_sb", [128, N_COLS])
        wsq_sb = sb("wsq_sb", [128, 4 * D])
        wmod_sb = sb("wmod_sb", [128, 6 * D])
        wlow_sb = sb("wlow_sb", [RANK, 4 * D])
        w1_sb = sb("w1_sb", [128, NETS, HIDDEN])
        w2_sb = sb("w2_sb", [128, NETS, HCH, D])
        sel_in = sb("sel_in", [128, STATES])
        ident_sb = sb("ident_sb", [128, 128])
        ident_bf = sb("ident_bf", [128, 128], BF16)
        sel_sb = sb("sel_sb", [128, STATES, 128], FP32R)
        m_dt = sb("m_dt", [128, D])
        m_c = sb("m_c", [128, D])
        a_pos = sb("a_pos", [128, STATES])
        a_neg = sb("a_neg", [128, STATES])
        b2_sum = sb("b2_sum", [128, 1])
        b2_gb = sb("b2_gb", [128, BATCH])
        c_silu = sb("c_silu", [128, BATCH])
        mod = sb("mod", [128, 6, BATCH])
        g_sign = sb("g_sign", [128, BATCH])
        g_size = sb("g_size", [128, BATCH])
        ones_col = sb("ones_col", [128, 1])
        half_neg = sb("half_neg", [128, BATCH * CHUNKS])
        eps_row = sb("eps_row", [128, CHUNKS])

        def col(name, i=0, n=1):
            return cols_sb[:, COLS[name][0] + i:COLS[name][0] + i + n]

        w_xc, w_z = wsq_sb[:, 0:D], wsq_sb[:, D:2 * D]
        w_out = wsq_sb[:, 2 * D:3 * D]
        w_b = wsq_sb[:, 3 * D:4 * D]

        x_res = sb("x_res", [128, BATCH * T])
        xs_all = sb("xs_all", [128, BATCH * T])
        zs_all = sb("zs_all", [128, BATCH * T])
        dt_two = sb("dt_two", [128, 2, T])
        u_two = sb("u_two", [128, 2, T])
        b_two = sb("b_two", [128, 2, T], FP32R)

        x_tok = sb("x_tok", [128, BATCH, CHUNKS, D])
        a_stats = sb("a_stats", [128, BATCH * CHUNKS, 6])
        a_mean = sb("a_mean", [128, BATCH * CHUNKS])
        a_diff = sb("a_diff", [128, BATCH * CHUNKS])
        a_var = sb("a_var", [128, BATCH * CHUNKS])
        a_rstd = sb("a_rstd", [128, BATCH * CHUNKS])
        x_norm = sb("x_norm", [128, 2, CHUNKS, D])
        h1 = sb("h1", [128, 2, T])
        conv = sb("conv", [128, 2, T])

        dt_log, dt_pos = conv[:, 0], conv[:, 1]
        y_sb, attn = h1[:, 0], h1[:, 1]
        x2_norm, x2_tok = x_norm[:, 0], x_tok[:, 0]
        a_ring = sb("a_ring", [128, RING, PER_UNIT, T])
        s_ring = sb("s_ring", [128, RING, PER_UNIT, T])
        s_acc = sb("s_acc", [128, PER_UNIT, T])
        s_sum = sb("s_sum", [128, T])
        dt_abs = sb("dt_abs", [128, T])
        x2 = sb("x2", [128, CHUNKS, 128])
        b_stats = sb("b_stats", [128, CHUNKS, 6])
        b_mv = sb("b_mv", [128, CHUNKS, 2])
        b_var = sb("b_var", [128, CHUNKS])
        b_rstd = sb("b_rstd", [128, CHUNKS])
        h2 = sb("h2", [128, NETS, T])
        g_max = sb("g_max", [128, CHUNKS])
        g_sub = sb("g_sub", [128, CHUNKS, EXPERTS])
        g_exp = sb("g_exp", [128, CHUNKS, EXPERTS])
        g_den = sb("g_den", [128, CHUNKS])
        g_inv = sb("g_inv", [128, CHUNKS])
        g_prob = sb("g_prob", [128, CHUNKS, EXPERTS])
        g_first = sb("g_first", [128, CHUNKS], BF16)
        g_ring = sb("g_ring", [128, G_RING, T])
        out_sb = sb("out_sb", [128, T])

        bank = ctx.enter_context(nc.psum_tensor("bank", [128, 8, 512], FP32))
        misc = bank[:, 7, :]
        net_out = bank[:, 6, :]

        ld_cols, ld_wsq, ld_wmod, ld_wlow = sem("ld_cols"), sem("ld_wsq"), sem("ld_wmod"), sem("ld_wlow")
        ld_w1, ld_w2, ld_sel, ld_ident, ld_xT = sem("ld_w1"), sem("ld_w2"), sem("ld_sel"), sem("ld_ident"), sem("ld_xT")
        ld_x = [sem("ld_x_first"), sem("ld_x_second"), sem("ld_x_rest")]
        consts_set, sel_done, ident_done, cond_done = sem("consts_set"), sem("sel_done"), sem("ident_done"), sem("cond_done")
        mod_mm, low_mm, mod_done, low_done = sem("mod_mm"), sem("low_mm"), sem("mod_done"), sem("low_done")
        a_exp_done, a_done, mod_step = sem("a_exp_done"), sem("a_done"), sem("mod_step")
        a_stats_done, a_sum_done = sem("a_stats_done"), sem("a_sum_done")
        a_rstd_done = sem("a_rstd_done")
        a_norm_done, a_xt_done, a_h_done = sem("a_norm_done"), sem("a_xt_done"), sem("a_h_done")
        xc_mm, z_mm, conv_mid, conv_done = sem("xc_mm"), sem("z_mm"), sem("conv_mid"), sem("conv_done")
        zs_done, xs_done = sem("zs_done"), sem("xs_done")
        b_mm, b_hi, b_lo, dt_mm = sem("b_mm"), sem("b_hi"), sem("b_lo"), sem("dt_mm")
        dt_act, dt_relu, dt_done, u_done = sem("dt_act"), sem("dt_relu"), sem("dt_done"), sem("u_done")
        b_cast, decay_done, bu_done, scan_done = sem("b_cast"), sem("decay_done"), sem("bu_done"), sem("scan_done")
        units_added, sum_done = sem("units_added"), sem("sum_done")
        c_mm, cs_done, y_done, o_mm, attn_done, x2_done = (sem("c_mm"), sem("cs_done"), sem("y_done"), sem("o_mm"),
                                                           sem("attn_done"), sem("x2_done"))
        x2t_mm, b_stats_done, b_mv_done = sem("x2t_mm"), sem("b_stats_done"), sem("b_mv_done")
        x2_tok_done = sem("x2_tok_done")
        b_var_done, b_rstd_done, b_norm_done = sem("b_var_done"), sem("b_rstd_done"), sem("b_norm_done")
        x2b_done, xn2t_mm, h2_done = sem("x2b_done"), sem("xn2t_mm"), sem("h2_done")
        gate_mm, gate_dve, gate_exp = sem("gate_mm"), sem("gate_dve"), sem("gate_exp")
        mask_mm, first_done, second_done = sem("mask_mm"), sem("first_done"), sem("second_done")
        hid_mm, hid_done, net_mm = sem("hid_mm"), sem("hid_done"), sem("net_mm")
        out_done, stored = sem("out_done"), sem("stored")

        MISC_FREED = {"b": (b_lo, 1, 1), "gate": (gate_dve, 6, 2), "c": (cs_done, 1, 1), "o": (attn_done, 1, 1),
                      "mask": (first_done, 1, 1), "dt": (dt_act, 3, 1), "x2t": (x2_tok_done, 1, 1),
                      "xn2t": (h2_done, 1, 1)}

        def seq(tile, b):
            return tile[:, bass.ds(b * T, T)]

        def settled(eng):
            eng.wait_ge(consts_set, 4)

        def units_released(i, k):
            k -= RING
            if k < 0:
                i, k = i - 1, k + UNITS
            return ADDS * i + max(k, 1)

        def stages(i):
            if not isinstance(i, int):
                return dict.fromkeys(("prepare", "scan", "mix", "experts", "finish"), True)
            return {n: 0 <= i + o < BATCH for n, o in
                    (("prepare", 1), ("scan", 0), ("mix", -1), ("experts", -2), ("finish", -3))}

        FIRST_LOOPED, END_LOOPED = 3, BATCH - 1
        GROUPS = [(0, 1), (1, 2), (2, BATCH)]

        def run_steps(eng, step):
            for i in range(-1, FIRST_LOOPED):
                step(i, i % 2)
            with eng.Fori(0, (END_LOOPED - FIRST_LOOPED) // 2) as q:
                for half in range(2):
                    step(FIRST_LOOPED + half + 2 * q, (FIRST_LOOPED + half) % 2)
            for i in range(END_LOOPED, BATCH + 3):
                step(i, i % 2)

        block = ctx.enter_context(nc.Block())

        @block.sync
        def _(sp):
            x_v = x.rearrange("b (c p) d -> p b c d", p=128)
            for (first, end), loaded in zip(GROUPS, ld_x):
                sp.dma_start(x_tok[:, first:end], x_v[:, first:end]).then_inc(loaded, 16)
                if first == 0:
                    sp.dma_start(ident_sb[:], ident).then_inc(ld_ident, 16)
                    sp.dma_start(wsq_sb[:], wsq).then_inc(ld_wsq, 16)
            sp.dma_start(wlow_sb[:], wlow).then_inc(ld_wlow, 16)
            sp.dma_start(sel_in[:], sel).then_inc(ld_sel, 16)
            sp.dma_start(x_res[:], xT).then_inc(ld_xT, 16)
            sp.dma_start(w1_sb[:], w1).then_inc(ld_w1, 16)
            sp.dma_start(w2_sb[:], w2).then_inc(ld_w2, 16)
            with sp.Fori(0, BATCH) as b:
                sp.wait_ge(out_done, b + 1)
                sp.dma_start(outT[:, bass.ds(b * T, T)], out_sb[:]).then_inc(stored, 16)
            sp.wait_ge(stored, 16 * BATCH)

        @block.tensor
        def _(pe):
            pe.wait_ge(ld_wmod, 16)
            pe.wait_ge(cond_done, 1)
            for m in range(6):
                last = nc.tensor.matmul(bank[:, 2, m * BATCH:(m + 1) * BATCH], wmod_sb[:, m * D:(m + 1) * D], c_silu[:],
                                        start=True, stop=True)
            last.then_inc(mod_mm, 1)

            def transposes(b, par):
                pe.wait_ge(a_norm_done, CHUNKS * b + CHUNKS)
                if not isinstance(b, int) or b >= 2:
                    pe.wait_ge(a_h_done, b - 1)
                for c in range(CHUNKS):
                    last = nc.tensor.transpose(bank[:, 4 + par, c * 128:(c + 1) * 128], x_norm[:, par, c], ident_sb[:])
                last.then_inc(a_xt_done, 1)

            def project(b, par):
                pe.wait_ge(a_h_done, b + 1)
                if not isinstance(b, int) or b >= 2:
                    pe.wait_ge(conv_done, 2 * b - 2)
                nc.tensor.matmul(bank[:, 6 + par], w_xc, h1[:, par], start=True, stop=True).then_inc(xc_mm, 1)
                if not isinstance(b, int) or b >= 2:
                    pe.wait_ge(zs_done, b - 1)
                nc.tensor.matmul(bank[:, par], w_z, h1[:, par], start=True, stop=True).then_inc(z_mm, 1)

            pe.wait_ge(ld_ident, 16)
            transposes(0, 0)
            pe.wait_ge(ld_wlow, 16)
            nc.tensor.matmul(bank[:, 3, 0:D], wlow_sb[:, 0:D], wlow_sb[:, D:2 * D], start=True, stop=True)
            nc.tensor.matmul(bank[:, 3, D:2 * D], wlow_sb[:, 2 * D:3 * D], wlow_sb[:, 3 * D:4 * D],
                             start=True, stop=True).then_inc(low_mm, 1)
            pe.wait_ge(ld_wsq, 16)
            transposes(1, 1)
            project(0, 0)
            with pe.Fori(0, BATCH // 2 - 1) as q:
                b = 2 * q + 1
                transposes(b + 1, 0)
                project(b, 1)
                transposes(b + 2, 1)
                project(b + 1, 0)
            project(BATCH - 1, 1)
            pe.wait_ge(conv_done, 2 * BATCH)
            pe.wait_ge(zs_done, BATCH)
            pe.wait_ge(low_done, 2)
            pe.wait_ge(mod_done, 1)
            pe.wait_ge(xs_done, BATCH)
            pe.wait_ge(sel_done, 1)
            pe.wait_ge(ident_done, 1)
            pe.wait_ge(ld_w1, 16)
            pe.wait_ge(ld_w2, 16)

            def misc_free(user, i):
                names = [n for n, _ in MISC_ORDER]
                at = names.index(user)
                if isinstance(i, int):
                    for n, (name, o) in enumerate(MISC_ORDER):
                        done = min(max(i + o + (n < at), 0), BATCH)
                        if done and name != user:
                            s, per, read = MISC_FREED[name]
                            pe.wait_ge(s, per * (done - 1) + read)
                else:
                    name, o = MISC_ORDER[at - 1]
                    s, per, read = MISC_FREED[name]
                    pe.wait_ge(s, per * (i + o - (at == 0)) + read)

            def step(i, par):
                on = stages(i)
                p, j, f = i + 1, i - 1, i - 2

                def hidden(t):
                    if t == 0:
                        pe.wait_ge(h2_done, f + 1)
                    if t == HCH:
                        pe.wait_ge(first_done, f + 1)
                    if t == 2 * HCH:
                        pe.wait_ge(second_done, f + 1)
                    n = TILES * f + t - 1
                    if not isinstance(f, int) or n > 0:
                        pe.wait_ge(hid_done, n)
                    e, m = divmod(t, HCH)
                    nc.tensor.matmul(bank[:, 4 + t % 2], w1_sb[:, e, m * 128:(m + 1) * 128], h2[:, e],
                                     start=True, stop=True).then_inc(hid_mm, 1)

                def output(t):
                    e, m = divmod(t, HCH)
                    if t == 0 and (not isinstance(f, int) or f > 0):
                        pe.wait_ge(out_done, f)
                    pe.wait_ge(hid_done, TILES * f + t + 1)
                    nc.tensor.matmul(net_out, w2_sb[:, e, m], g_ring[:, t % G_RING],
                                     start=(t == 0), stop=(t == TILES - 1)).then_inc(net_mm, 1)

                def experts_tiles(k):
                    for t in SLOT_TILES[k]:
                        hidden(t)
                        if t:
                            output(t - 1)
                    if k == UNITS - 1:
                        output(TILES - 1)

                for k in range(UNITS):
                    if on["scan"]:
                        if k == 0:
                            pe.wait_ge(b_lo, i + 1)
                        n = UNITS * i + k - 1
                        if not isinstance(i, int) or n > 0:
                            pe.wait_ge(scan_done, n)
                        for s in range(PER_UNIT):
                            last = nc.tensor.matmul(bank[:, PER_UNIT * (k % 2) + s], sel_sb[:, PER_UNIT * k + s],
                                                    b_two[:, par], start=True, stop=True)
                        last.then_inc(b_cast, 1)
                    if k == 0 and on["experts"]:
                        misc_free("mask", i)
                        pe.wait_ge(gate_dve, 6 * f + 6)
                        for c in range(CHUNKS):
                            last = nc.tensor.matmul(misc[:, c * 128:(c + 1) * 128],
                                                    g_first[:, c:c + 1].to_broadcast([128, 128]), ident_bf[:],
                                                    start=True, stop=True)
                        last.then_inc(mask_mm, 1)
                    if k == 1 and on["mix"]:
                        misc_free("c", i)
                        nc.tensor.matmul(misc, m_c[:], seq(xs_all, j), start=True, stop=True).then_inc(c_mm, 1)
                    if k == 2 and on["mix"]:
                        misc_free("o", i)
                        pe.wait_ge(y_done, j + 1)
                        nc.tensor.matmul(misc, w_out, y_sb, start=True, stop=True).then_inc(o_mm, 1)
                    if k == 3 and on["prepare"]:
                        misc_free("b", i)
                        nc.tensor.matmul(misc, w_b, seq(xs_all, p), start=True, stop=True).then_inc(b_mm, 1)
                    if k == 4 and on["mix"]:
                        misc_free("x2t", i)
                        pe.wait_ge(x2_done, j + 1)
                        for c in range(CHUNKS):
                            last = nc.tensor.transpose(misc[:, c * 128:(c + 1) * 128], x2[:, c], ident_sb[:])
                        last.then_inc(x2t_mm, 1)
                    if k == 5 and on["prepare"]:
                        misc_free("dt", i)
                        nc.tensor.matmul(misc, m_dt[:], seq(xs_all, p), start=True, stop=True).then_inc(dt_mm, 1)
                    if k == 6 and on["mix"]:
                        misc_free("xn2t", i)
                        pe.wait_ge(b_norm_done, CHUNKS * j + CHUNKS)
                        for c in range(CHUNKS):
                            last = nc.tensor.transpose(misc[:, c * 128:(c + 1) * 128], x2_norm[:, c], ident_sb[:])
                        last.then_inc(xn2t_mm, 1)
                    if k == 7 and on["mix"]:
                        misc_free("gate", i)
                        for c in range(CHUNKS):
                            last = nc.tensor.matmul(misc[:, EXPERTS * c:EXPERTS * (c + 1)], h2[:, 0, c * 128:(c + 1) * 128],
                                                    col("gate", 0, EXPERTS), start=True, stop=True)
                        last.then_inc(gate_mm, 1)
                    if on["experts"]:
                        experts_tiles(k)

            run_steps(pe, step)

        @block.scalar
        def _(act):
            act.dma_start(cols_sb[:], cols).then_inc(ld_cols, 16)
            act.dma_start(wmod_sb[:], wmod).then_inc(ld_wmod, 16)
            act.wait_ge(ld_cols, 16)
            nc.scalar.activation(c_silu[:], col("c", 0, BATCH), ACT.Silu).then_inc(cond_done, 1)

            def modulate(b, par):
                act.wait_ge(a_xt_done, b + 1)
                if not isinstance(b, int) or b >= 2:
                    act.wait_ge(z_mm, b - 1)
                settled(act)
                nc.scalar.activation(h1[:, par], bank[:, 4 + par], ACT.Identity, bias=mod[:, 0, bass.ds(b, 1)],
                                     scale=mod[:, 1, bass.ds(b, 1)]).then_inc(a_h_done, 1)

            def middle_tap_and_z(b, par):
                act.wait_ge(xc_mm, b + 1)
                if not isinstance(b, int) or b >= 2:
                    act.wait_ge(xs_done, b - 1)
                nc.scalar.activation(conv[:, par], bank[:, 6 + par], ACT.Copy, scale=col("conv", 1)).then_inc(conv_mid, 1)
                act.wait_ge(z_mm, b + 1)
                settled(act)
                nc.scalar.activation(seq(zs_all, b), bank[:, par], ACT.Silu).then_inc(zs_done, 1)

            def silu_conv(b, par):
                act.wait_ge(conv_done, 2 * b + 2)
                settled(act)
                nc.scalar.activation(seq(xs_all, b), conv[:, par], ACT.Silu).then_inc(xs_done, 1)

            act.wait_ge(mod_done, 1)
            modulate(0, 0)
            modulate(1, 1)
            middle_tap_and_z(0, 0)
            with act.Fori(0, BATCH // 2 - 1) as q:
                b = 2 * q + 1
                modulate(b + 1, 0)
                middle_tap_and_z(b, 1)
                silu_conv(b - 1, 0)
                modulate(b + 2, 1)
                middle_tap_and_z(b + 1, 0)
                silu_conv(b, 1)
            middle_tap_and_z(BATCH - 1, 1)
            silu_conv(BATCH - 2, 0)
            silu_conv(BATCH - 1, 1)
            nc.scalar.preload_act_table_set("natural_log_exp_and_others")
            nc.scalar.activation(a_pos[:], col("a_log", 0, STATES), ACT.Exp).then_inc(a_exp_done, 1)
            act.wait_ge(a_exp_done, 1)
            nc.scalar.activation(a_neg[:], a_pos[:], ACT.Copy, scale=-1.0).then_inc(a_done, 1)
            act.wait_ge(a_done, 1)
            act.wait_ge(consts_set, 4)

            def step(i, par):
                on = stages(i)
                p, j, f = i + 1, i - 1, i - 2
                for k in range(UNITS):
                    if on["scan"]:
                        if k == 0:
                            act.wait_ge(dt_done, i + 1)
                        n = UNITS * i + k - RING + 1
                        if not isinstance(i, int) or n > 0:
                            act.wait_ge(scan_done, n)
                        for s in range(PER_UNIT):
                            n = PER_UNIT * k + s
                            last = nc.scalar.activation(
                                a_ring[:, k % RING, s, 1:T], dt_two[:, par, 1:T], ACT.Exp,
                                scale=a_neg[:, n:n + 1])
                        last.then_inc(decay_done, 1)
                    if k == 3 and on["prepare"]:
                        act.wait_ge(b_mm, p + 1)
                        nc.scalar.activation(b_two[:, 1 - par], misc, ACT.Copy).then_inc(b_hi, 1)
                    if k == 4 and on["mix"]:
                        act.wait_ge(x2t_mm, j + 1)
                        if not isinstance(j, int) or j > 0:
                            act.wait_ge(b_norm_done, CHUNKS * j)
                        nc.scalar.activation(x2_tok.rearrange("p c d -> p (c d)"), misc, ACT.Copy).then_inc(x2_tok_done, 1)
                        act.wait_ge(x2_done, j + 1)
                        settled(act)
                        nc.scalar.activation(seq(x_res, j), x2[:].rearrange("p c t -> p (c t)"), ACT.Identity,
                                             bias=b2_gb[:, bass.ds(j, 1)]).then_inc(x2b_done, 1)
                    if k == 5 and on["prepare"]:
                        act.wait_ge(dt_mm, p + 1)
                        if not isinstance(p, int) or p > 0:
                            act.wait_ge(dt_done, p)
                        nc.scalar.activation(dt_pos, misc, ACT.Relu, bias=col("b_dt")).then_inc(dt_relu, 1)
                        nc.scalar.activation(dt_abs[:], misc, ACT.Abs, bias=col("b_dt")).then_inc(dt_act, 1)
                        act.wait_ge(dt_act, 3 * p + 1)
                        nc.scalar.activation(dt_abs[:], dt_abs[:], ACT.Exp, scale=-1.0).then_inc(dt_act, 1)
                        act.wait_ge(dt_act, 3 * p + 2)
                        nc.scalar.activation(dt_log, dt_abs[:], ACT.Ln, bias=ones_col[:]).then_inc(dt_act, 1)
                    if k == 6 and on["mix"]:
                        act.wait_ge(xn2t_mm, j + 1)
                        if not isinstance(j, int) or j > 0:
                            act.wait_ge(second_done, j)
                            act.wait_ge(hid_mm, TILES * (j - 1) + HCH)
                        settled(act)
                        nc.scalar.activation(h2[:, 0], misc, ACT.Identity, bias=mod[:, 3, bass.ds(j, 1)],
                                             scale=mod[:, 4, bass.ds(j, 1)]).then_inc(h2_done, 1)
                    if k == 7 and on["mix"]:
                        act.wait_ge(gate_dve, 6 * j + 2)
                        nc.scalar.activation(g_exp[:], g_sub[:], ACT.Exp).then_inc(gate_exp, 1)
                    if on["experts"]:
                        for t in SLOT_TILES[k]:
                            act.wait_ge(hid_mm, TILES * f + t + 1)
                            n = TILES * f + t - G_RING + 1
                            if not isinstance(f, int) or n > 0:
                                act.wait_ge(net_mm, n)
                            nc.scalar.activation(g_ring[:, t % G_RING], bank[:, 4 + t % 2], ACT.Relu,
                                                 bias=col("b1", t)).then_inc(hid_done, 1)

            run_steps(act, step)

        @block.vector
        def _(dve):
            nc.vector.memset(ones_col[:], 1.0).then_inc(consts_set, 1)
            nc.vector.memset(half_neg[:], -0.5).then_inc(consts_set, 1)
            nc.vector.memset(a_ring[:, :, :, 0:1], 0.0).then_inc(consts_set, 1)
            nc.vector.memset(eps_row[:], LN_EPS).then_inc(consts_set, 1)

            def statistics(n):
                first, end = GROUPS[n]
                dve.wait_ge(ld_x[n], 16)
                for b in range(first, end):
                    for c in range(CHUNKS):
                        last = nc.vector.bn_stats(a_stats[:, CHUNKS * b + c], x_tok[:, b, c])
                last.then_inc(a_stats_done, 1)
                g = slice(CHUNKS * first, CHUNKS * end)
                even, odd = a_stats[:, g, 0:3], a_stats[:, g, 3:6]
                dve.wait_ge(a_stats_done, n + 1)
                nc.vector.tensor_tensor(a_mean[:, g], even[:, :, 1], odd[:, :, 1], ALU.add)
                nc.vector.tensor_tensor(a_diff[:, g], even[:, :, 1], odd[:, :, 1], ALU.subtract)
                nc.vector.tensor_tensor(a_var[:, g], even[:, :, 2], odd[:, :, 2], ALU.add).then_inc(a_sum_done, 1)
                dve.wait_ge(a_sum_done, 3 * n + 1)
                nc.vector.tensor_scalar(a_mean[:, g], a_mean[:, g], 0.5, None, ALU.mult)
                nc.vector.tensor_scalar(a_var[:, g], a_var[:, g], 1.0 / D, LN_EPS, ALU.mult, ALU.add)
                nc.vector.scalar_tensor_tensor(a_diff[:, g], a_diff[:, g], 0.25, a_diff[:, g],
                                               ALU.mult, ALU.mult).then_inc(a_sum_done, 1)
                dve.wait_ge(a_sum_done, 3 * n + 2)
                nc.vector.tensor_tensor(a_var[:, g], a_var[:, g], a_diff[:, g], ALU.add).then_inc(a_sum_done, 1)

            def normalise(b, par):
                if not isinstance(b, int) or b >= 2:
                    dve.wait_ge(a_xt_done, b - 1)
                for c in range(CHUNKS):
                    stat = bass.ds(b * CHUNKS + c, 1)
                    nc.vector.tensor_scalar(x_norm[:, par, c], x_tok[:, bass.ds(b, 1), c], a_mean[:, stat],
                                            a_rstd[:, stat], ALU.subtract, ALU.mult).then_inc(a_norm_done, 1)

            def convolve(b, par):
                xc = bank[:, 6 + par]
                dve.wait_ge(conv_mid, b + 1)
                nc.vector.scalar_tensor_tensor(conv[:, par, 1:T], xc[:, 0:T - 1], col("conv", 0), conv[:, par, 1:T],
                                               ALU.mult, ALU.add).then_inc(conv_done, 1)
                dve.wait_ge(conv_done, 2 * b + 1)
                nc.vector.scalar_tensor_tensor(conv[:, par, 0:T - 1], xc[:, 1:T], col("conv", 2), conv[:, par, 0:T - 1],
                                               ALU.mult, ALU.add).then_inc(conv_done, 1)

            statistics(0)
            statistics(1)
            dve.wait_ge(mod_mm, 1)
            mps = bank[:, 2, 0:6 * BATCH].rearrange("p (m b) -> p m b", b=BATCH)
            nc.vector.tensor_copy(mod[:], mps).then_inc(mod_step, 1)
            dve.wait_ge(mod_step, 1)
            step_n = 1
            for m in (1, 4):
                nc.vector.tensor_scalar(mod[:, m], mod[:, m], 1.0, None, ALU.add).then_inc(mod_step, 1)
                step_n += 1
            for m in (2, 5):
                dve.wait_ge(mod_step, step_n)
                nc.vector.tensor_scalar(g_sign[:], mod[:, m], 0.0, 2.0, ALU.is_ge, ALU.mult).then_inc(mod_step, 1)
                nc.vector.tensor_scalar(g_size[:], mod[:, m], -1.0, GATE_FLOOR, ALU.mult, ALU.max).then_inc(mod_step, 1)
                step_n += 2
                dve.wait_ge(mod_step, step_n)
                nc.vector.tensor_tensor(g_size[:], mod[:, m], g_size[:], ALU.max).then_inc(mod_step, 1)
                step_n += 1
                dve.wait_ge(mod_step, step_n)
                nc.vector.scalar_tensor_tensor(mod[:, m], g_sign[:], -1.0, g_size[:], ALU.add, ALU.mult).then_inc(mod_step, 1)
                step_n += 1
            dve.wait_ge(mod_step, step_n)
            nc.vector.tensor_tensor(b2_sum[:], col("b2", 0), col("b2", 1), ALU.add).then_inc(mod_step, 1)
            dve.wait_ge(mod_step, step_n + 1)
            nc.vector.tensor_tensor(b2_sum[:], b2_sum[:], col("b2", 2), ALU.add).then_inc(mod_step, 1)
            dve.wait_ge(mod_step, step_n + 2)
            nc.vector.tensor_scalar(b2_gb[:], mod[:, 5], b2_sum[:], None, ALU.mult).then_inc(mod_done, 1)
            dve.wait_ge(a_rstd_done, 2)
            normalise(0, 0)
            normalise(1, 1)
            dve.wait_ge(low_mm, 1)
            nc.vector.tensor_copy(m_dt[:], bank[:, 3, 0:D]).then_inc(low_done, 1)
            nc.vector.tensor_copy(m_c[:], bank[:, 3, D:2 * D]).then_inc(low_done, 1)
            dve.wait_ge(ld_ident, 16)
            nc.vector.tensor_copy(ident_bf[:], ident_sb[:]).then_inc(ident_done, 1)
            statistics(2)
            dve.wait_ge(a_rstd_done, len(GROUPS))
            with dve.Fori(0, BATCH // 2 - 1) as q:
                for half in range(2):
                    normalise(2 * q + half + 2, half)
                    convolve(2 * q + half, half)
            convolve(BATCH - 2, 0)
            convolve(BATCH - 1, 1)

            def step(i, par):
                on = stages(i)
                p, j, f, w = i + 1, i - 1, i - 2, i - 3
                for k in range(UNITS):
                    pair = bank[:, PER_UNIT * (k % 2):PER_UNIT * (k % 2) + PER_UNIT]
                    if on["scan"]:
                        if k == 0:
                            dve.wait_ge(u_done, i + 1)
                        dve.wait_ge(b_cast, UNITS * i + k + 1)
                        u_rep = u_two[:, par].unsqueeze(1).to_broadcast([128, PER_UNIT, T])
                        nc.vector.tensor_tensor(pair, pair, u_rep, ALU.mult).then_inc(bu_done, 1)
                    if k == 0 and on["finish"]:
                        dve.wait_ge(net_mm, TILES * w + TILES)
                        dve.wait_ge(x2b_done, w + 1)
                        if not isinstance(w, int) or w > 0:
                            dve.wait_ge(stored, 16 * w)
                        nc.vector.scalar_tensor_tensor(out_sb[:], net_out, mod[:, 5, bass.ds(w, 1)], seq(x_res, w),
                                                       ALU.mult, ALU.add).then_inc(out_done, 1)
                    if k == 0 and on["experts"]:
                        dve.wait_ge(mask_mm, f + 1)
                        nc.vector.tensor_tensor(h2[:, 1], misc, h2[:, 0], ALU.mult).then_inc(first_done, 1)
                    if k == 1 and on["mix"]:
                        dve.wait_ge(c_mm, j + 1)
                        dve.wait_ge(sum_done, j + 1)
                        nc.vector.tensor_tensor(y_sb, misc, s_sum[:], ALU.mult).then_inc(cs_done, 1)
                        dve.wait_ge(cs_done, j + 1)
                        nc.vector.scalar_tensor_tensor(y_sb, seq(xs_all, j), col("d"), y_sb,
                                                       ALU.mult, ALU.add).then_inc(y_done, 1)
                    if k == 2 and on["mix"]:
                        dve.wait_ge(o_mm, j + 1)
                        nc.vector.scalar_tensor_tensor(attn, misc, mod[:, 2, bass.ds(j, 1)], seq(zs_all, j),
                                                       ALU.mult, ALU.mult).then_inc(attn_done, 1)
                    if k == 3 and on["prepare"]:
                        dve.wait_ge(b_hi, p + 1)
                        low = b_two[HALF:2 * HALF, 1 - par]
                        nc.vector.tensor_tensor(low, misc[HALF:2 * HALF], low, ALU.subtract).then_inc(b_lo, 1)
                    if k == 4 and on["mix"]:
                        dve.wait_ge(x2_tok_done, j + 1)
                        for c in range(CHUNKS):
                            nc.vector.bn_stats(b_stats[:, c], x2_tok[:, c]).then_inc(b_stats_done, 1)
                        dve.wait_ge(b_stats_done, CHUNKS * j + CHUNKS)
                    if k == 6 and on["prepare"]:
                        dve.wait_ge(dt_relu, p + 1)
                        dve.wait_ge(dt_act, 3 * p + 3)
                        nc.vector.scalar_tensor_tensor(dt_two[:, 1 - par], dt_log, DT_EPS, dt_pos,
                                                       ALU.add, ALU.add).then_inc(dt_done, 1)
                    if k == 7 and on["mix"]:
                        scores = misc[:, 0:EXPERTS * CHUNKS].rearrange("p (c e) -> p c e", e=EXPERTS)
                        dve.wait_ge(gate_mm, j + 1)
                        nc.vector.tensor_reduce(g_max[:], scores, AX, ALU.max).then_inc(gate_dve, 1)
                        dve.wait_ge(gate_dve, 6 * j + 1)
                        nc.vector.tensor_tensor(g_sub[:], scores, g_max[:].unsqueeze(2).to_broadcast([128, CHUNKS, EXPERTS]),
                                                ALU.subtract).then_inc(gate_dve, 1)
                    if on["scan"]:
                        dve.wait_ge(bu_done, UNITS * i + k + 1)
                        dve.wait_ge(decay_done, UNITS * i + k + 1)
                        n = units_released(i, k)
                        if not isinstance(i, int) or UNITS * i + k >= RING:
                            dve.wait_ge(units_added, n)
                        nc.vector.tensor_tensor_scan(
                            s_ring[:, k % RING].rearrange("p s t -> p (s t)"),
                            a_ring[:, k % RING].rearrange("p s t -> p (s t)"),
                            pair.rearrange("p s t -> p (s t)"), 0.0, ALU.mult, ALU.add).then_inc(scan_done, 1)
                    if k == 4 and on["mix"]:
                        for c in range(CHUNKS):
                            nc.vector.bn_aggr(b_mv[:, c], b_stats[:, c]).then_inc(b_mv_done, 1)
                    if k == 5 and on["mix"]:
                        dve.wait_ge(b_rstd_done, j + 1)
                        for c in range(CHUNKS):
                            nc.vector.tensor_scalar(x2_norm[:, c], x2_tok[:, c], b_mv[:, c, 0:1],
                                                    b_rstd[:, c:c + 1], ALU.subtract, ALU.mult).then_inc(b_norm_done, 1)
                    if k == 7 and on["mix"]:
                        dve.wait_ge(gate_exp, j + 1)
                        nc.vector.tensor_reduce(g_den[:], g_exp[:], AX, ALU.add).then_inc(gate_dve, 1)
                        dve.wait_ge(gate_dve, 6 * j + 3)
                        nc.vector.reciprocal(g_inv[:], g_den[:]).then_inc(gate_dve, 1)
                        dve.wait_ge(gate_dve, 6 * j + 4)
                        nc.vector.tensor_tensor(g_prob[:], g_exp[:], g_inv[:].unsqueeze(2).to_broadcast([128, CHUNKS, EXPERTS]),
                                                ALU.mult).then_inc(gate_dve, 1)
                        dve.wait_ge(gate_dve, 6 * j + 5)
                        nc.vector.tensor_tensor(g_first[:], g_prob[:, :, 0], g_prob[:, :, 1], ALU.is_ge).then_inc(gate_dve, 1)

            run_steps(dve, step)

        @block.gpsimd
        def _(pool):
            pool.wait_ge(consts_set, 4)

            for n, (first, end) in enumerate(GROUPS):
                g = slice(CHUNKS * first, CHUNKS * end)
                pool.wait_ge(a_sum_done, 3 * n + 3)
                nc.gpsimd.tensor_tensor(a_rstd[:, g], a_var[:, g], half_neg[:, g], ALU.pow).then_inc(a_rstd_done, 1)
            pool.wait_ge(ld_sel, 16)
            nc.gpsimd.tensor_copy(sel_sb[:], sel_in[:].unsqueeze(2).to_broadcast([128, STATES, 128])).then_inc(sel_done, 1)
            pool.wait_ge(xs_done, BATCH)
            pool.wait_ge(ld_xT, 16)

            def step(i, par):
                on = stages(i)
                p, j, f = i + 1, i - 1, i - 2
                for k in range(UNITS):
                    if k == 5 and on["mix"]:
                        pool.wait_ge(b_mv_done, CHUNKS * j + CHUNKS)
                        nc.gpsimd.tensor_tensor(b_var[:], b_mv[:, :, 1], eps_row[:], ALU.add).then_inc(b_var_done, 1)
                        pool.wait_ge(b_var_done, j + 1)
                        nc.gpsimd.tensor_tensor(b_rstd[:], b_var[:], half_neg[:, 0:CHUNKS], ALU.pow).then_inc(b_rstd_done, 1)
                    if on["scan"] and k:
                        pool.wait_ge(scan_done, UNITS * i + k + 1)
                        n = ADDS * i + k - 1
                        if not isinstance(i, int) or n > 0:
                            pool.wait_ge(units_added, n)
                        if k == 1 and (not isinstance(i, int) or i > 0):
                            pool.wait_ge(sum_done, i)
                        into = s_ring[:, 0] if k == 1 else s_acc[:]
                        nc.gpsimd.tensor_tensor(s_acc[:], into, s_ring[:, k % RING], ALU.add).then_inc(units_added, 1)
                    if k == 2 and on["mix"]:
                        pool.wait_ge(attn_done, j + 1)
                        if not isinstance(j, int) or j > 0:
                            pool.wait_ge(x2b_done, j)
                        nc.gpsimd.tensor_tensor(x2[:].rearrange("p c t -> p (c t)"), attn, seq(x_res, j),
                                                ALU.add).then_inc(x2_done, 1)
                    if k == 0 and on["experts"]:
                        pool.wait_ge(first_done, f + 1)
                        nc.gpsimd.tensor_tensor(h2[:, 2], h2[:, 0], h2[:, 1], ALU.subtract).then_inc(second_done, 1)
                    if k == 6 and on["prepare"]:
                        pool.wait_ge(dt_done, p + 1)
                        nc.gpsimd.tensor_tensor(u_two[:, 1 - par], dt_two[:, 1 - par], seq(xs_all, p), ALU.mult).then_inc(u_done, 1)
                if on["scan"]:
                    pool.wait_ge(units_added, ADDS * i + ADDS)
                    if not isinstance(i, int) or i > 0:
                        pool.wait_ge(cs_done, i)
                    nc.gpsimd.tensor_tensor(s_sum[:], s_acc[:, 0], s_acc[:, 1], ALU.add).then_inc(sum_done, 1)

            run_steps(pool, step)


def kernel(**inputs):
    import concourse.bacc as bacc
    from concourse.bass_utils import run_bass_kernel_spmd

    g = {k: np.asarray(v) for k, v in inputs.items()}

    def put(a):
        return np.ascontiguousarray(a)

    x = g["L0_attn_x"]
    w_x = g["L0_attn_W_x"]
    zeros = np.zeros((D, HALF - STATES), np.float32)
    b_rows = w_x[RANK:RANK + STATES].T
    w_c_pad = np.zeros((RANK, 2 * D), np.float32)
    w_c_pad[:STATES, :D] = w_x[RANK + STATES:]
    w_c_pad[:STATES, D:] = g["L0_attn_W_C"].T
    w1 = np.stack([g["L0_ffn_sw1"], *g["L0_ffn_w1"]], 1)
    w2 = np.stack([g["L0_ffn_sw2"], *g["L0_ffn_w2"]], 0)
    b1 = np.stack([g["L0_ffn_sb1"], *g["L0_ffn_b1"]], 0)
    b2 = np.stack([g["L0_ffn_sb2"], *g["L0_ffn_b2"]], 0)
    sel = np.zeros((128, STATES), np.float32)
    for n in range(STATES):
        sel[n, n] = sel[HALF + n, n] = 1.0
    arrays = {
        "x": x,
        "xT": x.reshape(BATCH * T, D).T,
        "cols": np.concatenate([g["L0_attn_conv_w"], g["L0_attn_b_dt"][:, None], g["L0_attn_A_log"],
                                g["L0_attn_D_param"][:, None], b1.reshape(TILES, 128).T, b2.T, g["L0_c"].T,
                                g["L0_ffn_gate_w"].T], 1),
        "wsq": np.concatenate([g["L0_attn_W_in"].T, g["L0_attn_W_out"].T, b_rows, zeros, b_rows, zeros,
                               np.zeros((D, 128 - 2 * HALF), np.float32)], 1),
        "wmod": g["L0_wmod"],
        "wlow": np.concatenate([w_x[:RANK], g["L0_attn_W_dt"].T, w_c_pad], 1),
        "w1": w1,
        "w2": w2.reshape(NETS, HCH, 128, D).transpose(2, 0, 1, 3),
        "sel": sel,
        "ident": np.eye(128, dtype=np.float32),
    }
    nc = bacc.Bacc("TRN2", target_bir_lowering=False, num_devices=1)
    arrays = {f"in_{k}": put(v) for k, v in arrays.items()}
    aps = [nc.dram_tensor(k, v.shape, mybir.dt.from_np(v.dtype), kind="ExternalInput").ap() for k, v in arrays.items()]
    outT = nc.dram_tensor("outT", (D, BATCH * T), FP32, kind="ExternalOutput").ap()
    adaln_kernel(nc, *aps, outT)
    r = run_bass_kernel_spmd(nc, [arrays], core_ids=[0])
    return put(r.results[0]["outT"].reshape(D, BATCH, T).transpose(1, 2, 0))
```

```python
from contextlib import ExitStack

import numpy as np

import concourse.bass as bass
from concourse import mybir

FP32 = mybir.dt.float32
FP32R = mybir.dt.float32r
BF16 = mybir.dt.bfloat16
ALU = mybir.AluOpType
ACT = mybir.ActivationFunctionType
AX = mybir.AxisListType.X

BATCH, T, D = 8, 512, 128
STATES, RANK, HIDDEN, EXPERTS = 16, 64, 512, 2
NETS = EXPERTS + 1
CHUNKS = T // 128
HCH = HIDDEN // 128
TILES = NETS * HCH
PER_UNIT = 2
UNITS = STATES // PER_UNIT
ADDS = UNITS - 1
HALF = 32
LN_EPS, DT_EPS, GATE_FLOOR = 1e-5, 1e-5, 0.25
RING = 4
G_RING = 3

COLS = {}
_at = 0
for _name, _n in (("conv", 3), ("b_dt", 1), ("a_log", STATES), ("d", 1), ("b1", TILES), ("b2", NETS),
                  ("c", BATCH), ("gate", EXPERTS)):
    COLS[_name] = (_at, _at + _n)
    _at += _n
N_COLS = _at

SLOT_TILES = [[2], [3, 4], [5], [6, 7], [8], [9, 10], [11], [0, 1]]
MASK_AFTER = SLOT_TILES[0][-1]
assert MASK_AFTER < HCH - 1 and sorted(sum(SLOT_TILES, [])) == list(range(TILES))

C_SLOTS = [(0, 0), (0, 1), (0, 2), (0, 4), (0, 6), (0, 7), (1, 0), (1, 1)]
DT_SLOTS = [(0, 0), (0, 1), (0, 3), (0, 5), (0, 6), (1, 0), (1, 3)]
DT_DIRECT = 2

MISC_ORDER = [("o", -1, 2), ("x2t", -1, 4), ("b", 1, 5), ("xn2t", -1, 6), ("gate", -1, 7)]


def adaln_kernel(nc, x, xT, cols, wsq, wmod, wlow, w1, w2, sel, ident, outT):
    ctx = ExitStack()
    with ctx:
        def sb(name, shape, dt=FP32):
            return ctx.enter_context(nc.sbuf_tensor(name, shape, dt))

        def sem(name):
            return ctx.enter_context(nc.semaphore(name))

        cols_sb = sb("cols_sb", [128, N_COLS])
        wsq_sb = sb("wsq_sb", [128, 4 * D])
        wmod_sb = sb("wmod_sb", [128, 6 * D])
        wlow_sb = sb("wlow_sb", [RANK, 4 * D])
        w1_sb = sb("w1_sb", [128, NETS, HIDDEN])
        w2_sb = sb("w2_sb", [128, NETS, HCH, D])
        sel_in = sb("sel_in", [128, STATES])
        ident_sb = sb("ident_sb", [128, 128])
        ident_bf = sb("ident_bf", [128, 128], BF16)
        sel_sb = sb("sel_sb", [128, STATES, 128], FP32R)
        m_dt = sb("m_dt", [128, D])
        m_c = sb("m_c", [128, D])
        a_pos = sb("a_pos", [128, STATES])
        a_neg = sb("a_neg", [128, STATES])
        b2_sum = sb("b2_sum", [128, 1])
        b2_gb = sb("b2_gb", [128, BATCH])
        c_silu = sb("c_silu", [128, BATCH])
        mod = sb("mod", [128, 6, BATCH])
        g_sign = sb("g_sign", [128, 2, BATCH])
        g_size = sb("g_size", [128, 2, BATCH])
        ones_col = sb("ones_col", [128, 1])
        half_neg = sb("half_neg", [128, BATCH * CHUNKS])
        eps_row = sb("eps_row", [128, CHUNKS])

        def col(name, i=0, n=1):
            return cols_sb[:, COLS[name][0] + i:COLS[name][0] + i + n]

        w_xc, w_z = wsq_sb[:, 0:D], wsq_sb[:, D:2 * D]
        w_out = wsq_sb[:, 2 * D:3 * D]
        w_b = wsq_sb[:, 3 * D:4 * D]

        x_res = sb("x_res", [128, BATCH * T])
        xs_all = sb("xs_all", [128, BATCH * T])
        zs_all = sb("zs_all", [128, BATCH * T])
        dt_two = sb("dt_two", [128, 2, T])
        u_two = sb("u_two", [128, 2, T])
        b_two = sb("b_two", [128, 2, T], FP32R)

        x_tok = sb("x_tok", [128, BATCH, CHUNKS, D])
        a_stats = sb("a_stats", [128, BATCH * CHUNKS, 6])
        a_mean = sb("a_mean", [128, BATCH * CHUNKS])
        a_diff = sb("a_diff", [128, BATCH * CHUNKS])
        a_var = sb("a_var", [128, BATCH * CHUNKS])
        a_rstd = sb("a_rstd", [128, BATCH * CHUNKS])
        x_norm = sb("x_norm", [128, 2, CHUNKS, D])
        h1 = sb("h1", [128, 2, T])
        conv = sb("conv", [128, 2, T])

        y_sb, attn = h1[:, 0], h1[:, 1]
        x2_norm = x_norm[:, 0]
        v_kept = sb("v_kept", [128, (BATCH - 1 - DT_DIRECT) * T])
        c_all = x_tok[:].rearrange("p b c d -> p (b c d)")
        a_ring = sb("a_ring", [128, RING, PER_UNIT, T])
        s_ring = sb("s_ring", [128, RING, PER_UNIT, T])
        s_acc = sb("s_acc", [128, PER_UNIT, T])
        s_sum = sb("s_sum", [128, T])
        dt_abs = sb("dt_abs", [128, T])
        dt_log = sb("dt_log", [128, T])
        dt_pos = sb("dt_pos", [128, T])
        x2_two = sb("x2_two", [128, 2, CHUNKS, 128])
        x2_tok = sb("x2_tok", [128, CHUNKS, D])
        b_stats = sb("b_stats", [128, CHUNKS, 6])
        b_mv = sb("b_mv", [128, CHUNKS, 2])
        b_var = sb("b_var", [128, CHUNKS])
        b_rstd = sb("b_rstd", [128, CHUNKS])
        mean_two = sb("mean_two", [128, CHUNKS])
        neg_mean = sb("neg_mean", [128, CHUNKS])
        b_shift = sb("b_shift", [128, CHUNKS])
        h2 = sb("h2", [128, NETS, T])
        g_max = sb("g_max", [128, CHUNKS])
        g_sub = sb("g_sub", [128, CHUNKS, EXPERTS])
        g_exp = sb("g_exp", [128, CHUNKS, EXPERTS])
        g_den = sb("g_den", [128, CHUNKS])
        g_inv = sb("g_inv", [128, CHUNKS])
        g_prob = sb("g_prob", [128, CHUNKS, EXPERTS])
        g_first = sb("g_first", [128, CHUNKS], BF16)
        g_ring = sb("g_ring", [128, G_RING, T])
        net_sb = sb("net_sb", [128, T])
        out_sb = sb("out_sb", [128, T])

        bank = ctx.enter_context(nc.psum_tensor("bank", [128, 8, 512], FP32))
        misc = bank[:, 7, :]
        net_out = bank[:, 6, :]

        ld_cols, ld_wsq, ld_wmod, ld_wlow = sem("ld_cols"), sem("ld_wsq"), sem("ld_wmod"), sem("ld_wlow")
        ld_w1, ld_w2, ld_sel, ld_ident, ld_xT = sem("ld_w1"), sem("ld_w2"), sem("ld_sel"), sem("ld_ident"), sem("ld_xT")
        ld_x = [sem("ld_x_0"), sem("ld_x_1"), sem("ld_x_2_3"), sem("ld_x_4_5"), sem("ld_x_6_7")]
        consts_set, sel_done, ident_done, cond_done = sem("consts_set"), sem("sel_done"), sem("ident_done"), sem("cond_done")
        mod_mm, low_mm, mod_done, low_done = sem("mod_mm"), sem("low_mm"), sem("mod_done"), sem("low_done")
        a_exp_done, a_done, mod_step = sem("a_exp_done"), sem("a_done"), sem("mod_step")
        a_stats_done, a_sum_done = sem("a_stats_done"), sem("a_sum_done")
        a_rstd_done = sem("a_rstd_done")
        a_norm_done, a_norm_pool = sem("a_norm_done"), sem("a_norm_pool")
        a_xt_done, a_h_done = sem("a_xt_done"), sem("a_h_done")
        xc_mm, z_mm, conv_mid, conv_done = sem("xc_mm"), sem("z_mm"), sem("conv_mid"), sem("conv_done")
        zs_done, xs_done = sem("zs_done"), sem("xs_done")
        b_mm, b_hi, b_lo, dt_mm = sem("b_mm"), sem("b_hi"), sem("b_lo"), sem("dt_mm")
        dt_act, dt_relu, dt_done, u_done = sem("dt_act"), sem("dt_relu"), sem("dt_done"), sem("u_done")
        b_cast, decay_done, bu_done, scan_done = sem("b_cast"), sem("decay_done"), sem("bu_done"), sem("scan_done")
        units_added, sum_done = sem("units_added"), sem("sum_done")
        c_mm, c_copied, v_copied = sem("c_mm"), sem("c_copied"), sem("v_copied")
        cs_done, y_done, o_mm, attn_done, x2_done = (sem("cs_done"), sem("y_done"), sem("o_mm"), sem("attn_done"),
                                                     sem("x2_done"))
        x2t_mm, b_stats_done, b_mv_done = sem("x2t_mm"), sem("b_stats_done"), sem("b_mv_done")
        x2_tok_done = sem("x2_tok_done")
        b_var_done, b_rstd_done, b_norm_done = sem("b_var_done"), sem("b_rstd_done"), sem("b_norm_done")
        xn2t_mm, h2_done = sem("xn2t_mm"), sem("h2_done")
        gate_mm, gate_dve, gate_exp = sem("gate_mm"), sem("gate_dve"), sem("gate_exp")
        mask_mm, first_done, second_done = sem("mask_mm"), sem("first_done"), sem("second_done")
        net_scaled = sem("net_scaled")
        hid_mm, hid_done, net_mm = sem("hid_mm"), sem("hid_done"), sem("net_mm")
        out_done, stored = sem("out_done"), sem("stored")

        MISC_FREED = {"b": (b_lo, 1, 1), "gate": (gate_dve, 6, 2), "o": (attn_done, 1, 1),
                      "x2t": (x2_tok_done, 1, 1),
                      "xn2t": (h2_done, 1, 1)}

        def seq(tile, b):
            return tile[:, bass.ds(b * T, T)]

        def settled(eng):
            eng.wait_ge(consts_set, 4)

        def hidden_bank(parity, t):
            return bank[:, 4 + (parity + t + (t > MASK_AFTER)) % 2]

        def mask_bank(parity):
            return bank[:, 4 + (parity + MASK_AFTER + 1) % 2]

        def add_residual(waits, engine, f, par):
            waits.wait_ge(net_scaled, f + 1)
            if not isinstance(f, int) or f > 0:
                waits.wait_ge(stored, 16 * f)
            engine.tensor_tensor(out_sb[:], net_sb[:], x2_two[:, par].rearrange("p c t -> p (c t)"),
                                 ALU.add).then_inc(out_done, 1)

        def units_released(i, k):
            k -= RING
            if k < 0:
                i, k = i - 1, k + UNITS
            return ADDS * i + max(k, 1)

        def stages(i):
            if not isinstance(i, int):
                return dict.fromkeys(("prepare", "scan", "mix", "experts"), True)
            return {n: 0 <= i + o < BATCH for n, o in
                    (("prepare", 1), ("scan", 0), ("mix", -1), ("experts", -2))}

        FIRST_LOOPED, END_LOOPED = 3, BATCH - 1
        GROUPS = [(0, 1), (1, 2), (2, 4), (4, 6), (6, 8)]
        assert GROUPS[-1][1] == BATCH

        def run_steps(eng, step):
            for i in range(FIRST_LOOPED):
                step(i, i % 2)
            with eng.Fori(0, (END_LOOPED - FIRST_LOOPED) // 2) as q:
                for half in range(2):
                    step(FIRST_LOOPED + half + 2 * q, (FIRST_LOOPED + half) % 2)
            for i in range(END_LOOPED, BATCH + 2):
                step(i, i % 2)

        block = ctx.enter_context(nc.Block())

        @block.sync
        def _(sp):
            x_v = x.rearrange("b (c p) d -> p b c d", p=128)
            for (first, end), loaded in zip(GROUPS, ld_x):
                sp.dma_start(x_tok[:, first:end], x_v[:, first:end]).then_inc(loaded, 16)
                if first == 0:
                    sp.dma_start(ident_sb[:], ident).then_inc(ld_ident, 16)
                    sp.dma_start(wsq_sb[:], wsq).then_inc(ld_wsq, 16)
            sp.dma_start(wlow_sb[:], wlow).then_inc(ld_wlow, 16)
            sp.dma_start(x_res[:], xT).then_inc(ld_xT, 16)
            sp.dma_start(w1_sb[:], w1).then_inc(ld_w1, 16)
            sp.dma_start(w2_sb[:], w2).then_inc(ld_w2, 16)
            with sp.Fori(0, BATCH) as b:
                sp.wait_ge(out_done, b + 1)
                sp.dma_start(outT[:, bass.ds(b * T, T)], out_sb[:]).then_inc(stored, 16)
            sp.wait_ge(stored, 16 * BATCH)

        @block.tensor
        def _(pe):
            pe.wait_ge(ld_wmod, 16)
            pe.wait_ge(cond_done, 1)
            for m in range(6):
                last = nc.tensor.matmul(bank[:, 2, m * BATCH:(m + 1) * BATCH], wmod_sb[:, m * D:(m + 1) * D], c_silu[:],
                                        start=True, stop=True)
            last.then_inc(mod_mm, 1)

            def transposes(b, par, normalised, count):
                pe.wait_ge(normalised, count)
                if not isinstance(b, int) or b >= 2:
                    pe.wait_ge(a_h_done, b - 1)
                for c in range(CHUNKS):
                    last = nc.tensor.transpose(bank[:, 4 + par, c * 128:(c + 1) * 128], x_norm[:, par, c], ident_sb[:])
                last.then_inc(a_xt_done, 1)

            def project(b, par):
                pe.wait_ge(a_h_done, b + 1)
                if not isinstance(b, int) or b >= 2:
                    pe.wait_ge(conv_done, 2 * b - 2)
                nc.tensor.matmul(bank[:, 6 + par], w_xc, h1[:, par], start=True, stop=True).then_inc(xc_mm, 1)
                if not isinstance(b, int) or b >= 2:
                    pe.wait_ge(zs_done, b - 1)
                nc.tensor.matmul(bank[:, par], w_z, h1[:, par], start=True, stop=True).then_inc(z_mm, 1)

            pe.wait_ge(ld_ident, 16)
            transposes(0, 0, a_norm_done, CHUNKS)
            pe.wait_ge(ld_wlow, 16)
            nc.tensor.matmul(bank[:, 3, 0:D], wlow_sb[:, 0:D], wlow_sb[:, D:2 * D], start=True, stop=True)
            nc.tensor.matmul(bank[:, 3, D:2 * D], wlow_sb[:, 2 * D:3 * D], wlow_sb[:, 3 * D:4 * D],
                             start=True, stop=True).then_inc(low_mm, 1)
            pe.wait_ge(ld_wsq, 16)
            transposes(1, 1, a_norm_done, 2 * CHUNKS)
            project(0, 0)

            def pair(q):
                b = 2 * q + 1
                transposes(b + 1, 0, a_norm_done, CHUNKS * (q + 3))
                project(b, 1)
                transposes(b + 2, 1, a_norm_pool, 2 * (q + 1))
                project(b + 1, 0)

            with pe.Fori(0, BATCH // 2 - 2) as q:
                pair(q)
            pe.wait_ge(mod_done, 1)
            pe.wait_ge(low_done, 2)
            pe.wait_ge(xs_done, 1)
            nc.tensor.matmul(bank[:, 2], w_b, seq(xs_all, 0), start=True, stop=True).then_inc(b_mm, 1)
            nc.tensor.matmul(bank[:, 3], m_dt[:], seq(xs_all, 0), start=True, stop=True).then_inc(dt_mm, 1)
            pair(BATCH // 2 - 2)
            project(BATCH - 1, 1)
            pe.wait_ge(zs_done, BATCH)
            pe.wait_ge(dt_relu, 1)
            pe.wait_ge(dt_act, 1)
            pe.wait_ge(sel_done, 1)
            pe.wait_ge(ident_done, 1)
            pe.wait_ge(ld_w1, 16)
            pe.wait_ge(ld_w2, 16)

            def misc_free(user, i):
                at = [name for name, _, _ in MISC_ORDER].index(user)
                if isinstance(i, int):
                    pe.wait_ge(c_copied, sum(at_slot < (i, MISC_ORDER[at][2]) for at_slot in C_SLOTS))
                    for n, (name, o, _) in enumerate(MISC_ORDER):
                        done = min(max(i + o + (n < at), 0), BATCH)
                        if done and name != user:
                            s, per, read = MISC_FREED[name]
                            pe.wait_ge(s, per * (done - 1) + read)
                else:
                    name, o, _ = MISC_ORDER[at - 1]
                    s, per, read = MISC_FREED[name]
                    pe.wait_ge(s, per * (i + o - (at == 0)) + read)

            def c_projection(i, k):
                b = C_SLOTS.index((i, k))
                if b == 0:
                    pe.wait_ge(conv_done, 2 * BATCH)
                    pe.wait_ge(xs_done, BATCH)
                else:
                    pe.wait_ge(c_copied, b)
                pe.wait_ge(b_lo, i + 1 + (k > 5))
                nc.tensor.matmul(misc, m_c[:], seq(xs_all, b), start=True, stop=True).then_inc(c_mm, 1)

            def dt_projection(i, k):
                n = DT_SLOTS.index((i, k))
                if n == 0:
                    pe.wait_ge(a_h_done, BATCH)
                    pe.wait_ge(conv_done, 2 * BATCH)
                    pe.wait_ge(xs_done, BATCH)
                if n > DT_DIRECT:
                    pe.wait_ge(v_copied, n - DT_DIRECT)
                nc.tensor.matmul(bank[:, 4 + min(n, DT_DIRECT)], m_dt[:], seq(xs_all, n + 1),
                                 start=True, stop=True).then_inc(dt_mm, 1)

            def step(i, par):
                on = stages(i)
                p, j, f = i + 1, i - 1, i - 2

                def hidden(b, parity, t):
                    if t == 0:
                        if isinstance(b, int) and b == 0:
                            pe.wait_ge(dt_act, 3 * DT_DIRECT + 1)
                            pe.wait_ge(v_copied, len(DT_SLOTS) - DT_DIRECT)
                        pe.wait_ge(h2_done, b + 1)
                    if t == min(HCH, MASK_AFTER + 2):
                        pe.wait_ge(first_done, b + 1)
                    if t == 2 * HCH:
                        pe.wait_ge(second_done, b + 1)
                    n = TILES * b + t - (t != MASK_AFTER + 1)
                    if not isinstance(b, int) or n > 0:
                        pe.wait_ge(hid_done, n)
                    e, m = divmod(t, HCH)
                    nc.tensor.matmul(hidden_bank(parity, t), w1_sb[:, e, m * 128:(m + 1) * 128], h2[:, e],
                                     start=True, stop=True).then_inc(hid_mm, 1)

                def output(b, t):
                    e, m = divmod(t, HCH)
                    if t == 0 and (not isinstance(b, int) or b > 0):
                        pe.wait_ge(net_scaled, b)
                    pe.wait_ge(hid_done, TILES * b + t + 1)
                    nc.tensor.matmul(net_out, w2_sb[:, e, m], g_ring[:, t % G_RING],
                                     start=(t == 0), stop=(t == TILES - 1)).then_inc(net_mm, 1)

                def experts_tiles(b, parity, k):
                    for t in SLOT_TILES[k]:
                        hidden(b, parity, t)
                        if t:
                            output(b, t - 1)
                    if t == TILES - 1:
                        output(b, t)

                for k in range(UNITS):
                    if on["scan"]:
                        if k == 0:
                            pe.wait_ge(b_lo, i + 1)
                        n = UNITS * i + k - 1
                        if not isinstance(i, int) or n > 0:
                            pe.wait_ge(scan_done, n)
                        for s in range(PER_UNIT):
                            last = nc.tensor.matmul(bank[:, PER_UNIT * (k % 2) + s], sel_sb[:, PER_UNIT * k + s],
                                                    b_two[:, par], start=True, stop=True)
                        last.then_inc(b_cast, 1)
                    if isinstance(i, int) and (i, k) in DT_SLOTS:
                        dt_projection(i, k)
                    if isinstance(i, int) and (i, k) in C_SLOTS:
                        c_projection(i, k)
                    if k == 2 and on["mix"]:
                        misc_free("o", i)
                        pe.wait_ge(y_done, j + 1)
                        nc.tensor.matmul(misc, w_out, y_sb, start=True, stop=True).then_inc(o_mm, 1)
                    if k == 4 and on["mix"]:
                        misc_free("x2t", i)
                        pe.wait_ge(x2_done, j + 1)
                        for c in range(CHUNKS):
                            last = nc.tensor.transpose(misc[:, c * 128:(c + 1) * 128], x2_two[:, 1 - par, c], ident_sb[:])
                        last.then_inc(x2t_mm, 1)
                    if k == 5 and on["prepare"]:
                        misc_free("b", i)
                        nc.tensor.matmul(misc, w_b, seq(xs_all, p), start=True, stop=True).then_inc(b_mm, 1)
                    if k == 6 and on["mix"]:
                        misc_free("xn2t", i)
                        pe.wait_ge(b_norm_done, CHUNKS * j + CHUNKS)
                        for c in range(CHUNKS):
                            last = nc.tensor.transpose(misc[:, c * 128:(c + 1) * 128], x2_norm[:, c], ident_sb[:])
                        last.then_inc(xn2t_mm, 1)
                    if k == 7 and on["mix"]:
                        misc_free("gate", i)
                        for c in range(CHUNKS):
                            last = nc.tensor.matmul(misc[:, EXPERTS * c:EXPERTS * (c + 1)], h2[:, 0, c * 128:(c + 1) * 128],
                                                    col("gate", 0, EXPERTS), start=True, stop=True)
                        last.then_inc(gate_mm, 1)
                    if k < UNITS - 1 and on["experts"]:
                        experts_tiles(f, par, k)
                    if k == 0 and on["experts"]:
                        pe.wait_ge(hid_done, TILES * f + MASK_AFTER)
                        pe.wait_ge(gate_dve, 6 * f + 6)
                        mask = mask_bank(par)
                        for c in range(CHUNKS):
                            last = nc.tensor.matmul(mask[:, c * 128:(c + 1) * 128],
                                                    g_first[:, c:c + 1].to_broadcast([128, 128]), ident_bf[:],
                                                    start=True, stop=True)
                        last.then_inc(mask_mm, 1)
                    if k == UNITS - 1 and on["mix"]:
                        experts_tiles(j, 1 - par, k)

            run_steps(pe, step)

        @block.scalar
        def _(act):
            act.dma_start(cols_sb[:], cols).then_inc(ld_cols, 16)
            act.dma_start(wmod_sb[:], wmod).then_inc(ld_wmod, 16)
            act.dma_start(sel_in[:], sel).then_inc(ld_sel, 16)
            act.wait_ge(ld_cols, 16)
            nc.scalar.activation(c_silu[:], col("c", 0, BATCH), ACT.Silu).then_inc(cond_done, 1)
            act.wait_ge(ld_sel, 16)
            nc.scalar.activation(sel_sb[:], sel_in[:].unsqueeze(2).to_broadcast([128, STATES, 128]), ACT.Copy).then_inc(sel_done, 1)

            def modulate(b, par):
                act.wait_ge(a_xt_done, b + 1)
                if not isinstance(b, int) or b >= 2:
                    act.wait_ge(z_mm, b - 1)
                settled(act)
                nc.scalar.activation(h1[:, par], bank[:, 4 + par], ACT.Identity, bias=mod[:, 0, bass.ds(b, 1)],
                                     scale=mod[:, 1, bass.ds(b, 1)]).then_inc(a_h_done, 1)

            def middle_tap_and_z(b, par):
                act.wait_ge(xc_mm, b + 1)
                if not isinstance(b, int) or b >= 2:
                    act.wait_ge(xs_done, b - 1)
                nc.scalar.activation(conv[:, par], bank[:, 6 + par], ACT.Copy, scale=col("conv", 1)).then_inc(conv_mid, 1)
                act.wait_ge(z_mm, b + 1)
                settled(act)
                nc.scalar.activation(seq(zs_all, b), bank[:, par], ACT.Silu).then_inc(zs_done, 1)

            def silu_conv(b, par):
                act.wait_ge(conv_done, 2 * b + 2)
                settled(act)
                nc.scalar.activation(seq(xs_all, b), conv[:, par], ACT.Silu).then_inc(xs_done, 1)

            def split_b(p, par, projected):
                act.wait_ge(b_mm, p + 1)
                nc.scalar.activation(b_two[:, par], projected, ACT.Copy).then_inc(b_hi, 1)

            def dt_parts(p, projected):
                if not isinstance(p, int) or p > 0:
                    act.wait_ge(dt_done, p)
                if isinstance(p, int) and p <= DT_DIRECT:
                    act.wait_ge(dt_mm, p + 1)
                else:
                    act.wait_ge(v_copied, len(DT_SLOTS) - DT_DIRECT)
                nc.scalar.activation(dt_pos[:], projected, ACT.Relu, bias=col("b_dt")).then_inc(dt_relu, 1)
                nc.scalar.activation(dt_abs[:], projected, ACT.Abs, bias=col("b_dt")).then_inc(dt_act, 1)

            def dt_logarithm(p):
                act.wait_ge(dt_act, 3 * p + 1)
                nc.scalar.activation(dt_abs[:], dt_abs[:], ACT.Exp, scale=-1.0).then_inc(dt_act, 1)
                act.wait_ge(dt_act, 3 * p + 2)
                nc.scalar.activation(dt_log[:], dt_abs[:], ACT.Ln, bias=ones_col[:]).then_inc(dt_act, 1)

            def normalise_x2(j):
                act.wait_ge(b_rstd_done, 2 * j + 2)
                for c in range(CHUNKS):
                    nc.scalar.activation(x2_norm[:, c], x2_tok[:, c], ACT.Identity, bias=b_shift[:, c:c + 1],
                                         scale=b_rstd[:, c:c + 1]).then_inc(b_norm_done, 1)

            def decays(i, k, par):
                if k == 0:
                    act.wait_ge(dt_done, i + 1)
                n = UNITS * i + k - RING + 1
                if not isinstance(i, int) or n > 0:
                    act.wait_ge(scan_done, n)
                for s in range(PER_UNIT):
                    n = PER_UNIT * k + s
                    last = nc.scalar.activation(a_ring[:, k % RING, s, 1:T], dt_two[:, par, 1:T], ACT.Exp,
                                                scale=a_neg[:, n:n + 1])
                last.then_inc(decay_done, 1)

            act.wait_ge(mod_done, 1)
            modulate(0, 0)
            modulate(1, 1)
            middle_tap_and_z(0, 0)

            def pair(q):
                b = 2 * q + 1
                modulate(b + 1, 0)
                middle_tap_and_z(b, 1)
                silu_conv(b - 1, 0)
                modulate(b + 2, 1)
                middle_tap_and_z(b + 1, 0)
                silu_conv(b, 1)

            with act.Fori(0, BATCH // 2 - 2) as q:
                pair(q)
            split_b(0, 0, bank[:, 2])
            pair(BATCH // 2 - 2)
            middle_tap_and_z(BATCH - 1, 1)
            silu_conv(BATCH - 2, 0)
            dt_parts(0, bank[:, 3])
            silu_conv(BATCH - 1, 1)
            nc.scalar.preload_act_table_set("natural_log_exp_and_others")
            dt_logarithm(0)
            nc.scalar.activation(a_pos[:], col("a_log", 0, STATES), ACT.Exp).then_inc(a_exp_done, 1)
            act.wait_ge(a_exp_done, 1)
            nc.scalar.activation(a_neg[:], a_pos[:], ACT.Copy, scale=-1.0).then_inc(a_done, 1)
            act.wait_ge(a_done, 1)
            act.wait_ge(consts_set, 4)
            decays(0, 0, 0)

            def step(i, par):
                on = stages(i)
                p, j, f = i + 1, i - 1, i - 2
                for k in range(UNITS):
                    if isinstance(i, int) and (i, k) in C_SLOTS:
                        b = C_SLOTS.index((i, k))
                        act.wait_ge(c_mm, b + 1)
                        nc.scalar.activation(seq(c_all, b), misc, ACT.Copy).then_inc(c_copied, 1)
                    if k == 7 and on["experts"]:
                        act.wait_ge(net_mm, TILES * f + TILES)
                        if not isinstance(f, int) or f > 0:
                            act.wait_ge(out_done, f)
                        settled(act)
                        nc.scalar.activation(net_sb[:], net_out, ACT.Identity, bias=b2_gb[:, bass.ds(f, 1)],
                                             scale=mod[:, 5, bass.ds(f, 1)]).then_inc(net_scaled, 1)
                    if isinstance(i, int) and (i, k) in DT_SLOTS[DT_DIRECT:]:
                        n = DT_SLOTS.index((i, k))
                        act.wait_ge(dt_mm, n + 2)
                        nc.scalar.activation(seq(v_kept, n - DT_DIRECT), bank[:, 4 + DT_DIRECT], ACT.Copy).then_inc(v_copied, 1)
                    if k == 3 and on["prepare"]:
                        direct = isinstance(p, int) and p <= DT_DIRECT
                        dt_parts(p, bank[:, 3 + p] if direct else seq(v_kept, p - DT_DIRECT - 1))
                    if k == 4 and on["mix"]:
                        act.wait_ge(x2t_mm, j + 1)
                        if not isinstance(j, int) or j > 0:
                            act.wait_ge(b_norm_done, CHUNKS * j)
                        nc.scalar.activation(x2_tok[:].rearrange("p c d -> p (c d)"), misc, ACT.Copy).then_inc(x2_tok_done, 1)
                    if k == 5 and on["prepare"]:
                        split_b(p, 1 - par, misc)
                    if k == 7 and on["mix"]:
                        act.wait_ge(gate_dve, 6 * j + 2)
                        nc.scalar.activation(g_exp[:], g_sub[:], ACT.Exp).then_inc(gate_exp, 1)
                    if k == 5 and on["mix"] and not on["experts"]:
                        normalise_x2(j)
                    if on["experts" if k < UNITS - 1 else "mix"]:
                        b, parity = (f, par) if k < UNITS - 1 else (j, 1 - par)
                        for t in SLOT_TILES[k]:
                            act.wait_ge(hid_mm, TILES * b + t + 1)
                            n = TILES * b + t - G_RING + 1
                            if not isinstance(b, int) or n > 0:
                                act.wait_ge(net_mm, n)
                            nc.scalar.activation(g_ring[:, t % G_RING], hidden_bank(parity, t), ACT.Relu,
                                                 bias=col("b1", t)).then_inc(hid_done, 1)
                            if k == 5 and on["mix"] and t == SLOT_TILES[k][0]:
                                normalise_x2(j)
                    if k == 6 and on["mix"]:
                        act.wait_ge(xn2t_mm, j + 1)
                        if not isinstance(j, int) or j > 0:
                            act.wait_ge(second_done, j)
                            act.wait_ge(hid_mm, TILES * j - TILES + HCH)
                        settled(act)
                        nc.scalar.activation(h2[:, 0], misc, ACT.Identity, bias=mod[:, 3, bass.ds(j, 1)],
                                             scale=mod[:, 4, bass.ds(j, 1)]).then_inc(h2_done, 1)
                    if k == 4 and on["prepare"]:
                        dt_logarithm(p)
                    if k < UNITS - 1 and on["scan"]:
                        decays(i, k + 1, par)
                    if k == UNITS - 1 and on["prepare"]:
                        decays(p, 0, 1 - par)

            run_steps(act, step)

        @block.vector
        def _(dve):
            nc.vector.memset(ones_col[:], 1.0).then_inc(consts_set, 1)
            nc.vector.memset(half_neg[:], -0.5).then_inc(consts_set, 1)
            nc.vector.memset(a_ring[:, :, :, 0:1], 0.0).then_inc(consts_set, 1)
            nc.vector.memset(eps_row[:], LN_EPS).then_inc(consts_set, 1)

            def statistics(n):
                first, end = GROUPS[n]
                dve.wait_ge(ld_x[n], 16)
                for b in range(first, end):
                    for c in range(CHUNKS):
                        last = nc.vector.bn_stats(a_stats[:, CHUNKS * b + c], x_tok[:, b, c])
                last.then_inc(a_stats_done, 1)
                g = slice(CHUNKS * first, CHUNKS * end)
                even, odd = a_stats[:, g, 0:3], a_stats[:, g, 3:6]
                dve.wait_ge(a_stats_done, n + 1)
                nc.vector.tensor_tensor(a_mean[:, g], even[:, :, 1], odd[:, :, 1], ALU.add)
                nc.vector.tensor_tensor(a_diff[:, g], even[:, :, 1], odd[:, :, 1], ALU.subtract)
                nc.vector.tensor_tensor(a_var[:, g], even[:, :, 2], odd[:, :, 2], ALU.add).then_inc(a_sum_done, 1)
                dve.wait_ge(a_sum_done, 3 * n + 1)
                nc.vector.tensor_scalar(a_mean[:, g], a_mean[:, g], 0.5, None, ALU.mult)
                nc.vector.tensor_scalar(a_var[:, g], a_var[:, g], 1.0 / D, LN_EPS, ALU.mult, ALU.add)
                nc.vector.scalar_tensor_tensor(a_diff[:, g], a_diff[:, g], 0.25, a_diff[:, g],
                                               ALU.mult, ALU.mult).then_inc(a_sum_done, 1)
                dve.wait_ge(a_sum_done, 3 * n + 2)
                nc.vector.tensor_tensor(a_var[:, g], a_var[:, g], a_diff[:, g], ALU.add).then_inc(a_sum_done, 1)

            def normalise(b, par):
                if not isinstance(b, int) or b >= 2:
                    dve.wait_ge(a_xt_done, b - 1)
                for c in range(CHUNKS):
                    stat = bass.ds(b * CHUNKS + c, 1)
                    nc.vector.tensor_scalar(x_norm[:, par, c], x_tok[:, bass.ds(b, 1), c], a_mean[:, stat],
                                            a_rstd[:, stat], ALU.subtract, ALU.mult).then_inc(a_norm_done, 1)

            def convolve(b, par):
                xc = bank[:, 6 + par]
                dve.wait_ge(conv_mid, b + 1)
                nc.vector.scalar_tensor_tensor(conv[:, par, 1:T], xc[:, 0:T - 1], col("conv", 0), conv[:, par, 1:T],
                                               ALU.mult, ALU.add).then_inc(conv_done, 1)
                dve.wait_ge(conv_done, 2 * b + 1)
                nc.vector.scalar_tensor_tensor(conv[:, par, 0:T - 1], xc[:, 1:T], col("conv", 2), conv[:, par, 0:T - 1],
                                               ALU.mult, ALU.add).then_inc(conv_done, 1)

            def b_low(p, par, projected):
                dve.wait_ge(b_hi, p + 1)
                low = b_two[HALF:2 * HALF, par]
                nc.vector.tensor_tensor(low, projected[HALF:2 * HALF], low, ALU.subtract).then_inc(b_lo, 1)

            def dt_sum(p, par):
                dve.wait_ge(dt_relu, p + 1)
                dve.wait_ge(dt_act, 3 * p + 3)
                nc.vector.scalar_tensor_tensor(dt_two[:, par], dt_log[:], DT_EPS, dt_pos[:],
                                               ALU.add, ALU.add).then_inc(dt_done, 1)

            statistics(0)
            dve.wait_ge(a_rstd_done, 1)
            normalise(0, 0)
            statistics(1)
            dve.wait_ge(mod_mm, 1)
            mps = bank[:, 2, 0:6 * BATCH].rearrange("p (m b) -> p m b", b=BATCH)
            nc.vector.tensor_copy(mod[:], mps).then_inc(mod_step, 1)
            nc.vector.tensor_tensor(b2_sum[:], col("b2", 0), col("b2", 1), ALU.add).then_inc(mod_step, 1)
            dve.wait_ge(mod_step, 2)
            gates, scales = mod[:, 2:6:3], mod[:, 1:5:3]
            nc.vector.tensor_scalar(scales, scales, 1.0, None, ALU.add).then_inc(mod_step, 1)
            nc.vector.tensor_scalar(g_sign[:], gates, 0.0, 2.0, ALU.is_ge, ALU.mult).then_inc(mod_step, 1)
            nc.vector.tensor_scalar(g_size[:], gates, -1.0, GATE_FLOOR, ALU.mult, ALU.max).then_inc(mod_step, 1)
            nc.vector.tensor_tensor(b2_sum[:], b2_sum[:], col("b2", 2), ALU.add).then_inc(mod_step, 1)
            dve.wait_ge(mod_step, 6)
            nc.vector.tensor_tensor(g_size[:], gates, g_size[:], ALU.max).then_inc(mod_step, 1)
            dve.wait_ge(mod_step, 7)
            nc.vector.scalar_tensor_tensor(gates, g_sign[:], -1.0, g_size[:], ALU.add, ALU.mult).then_inc(mod_step, 1)
            dve.wait_ge(mod_step, 8)
            nc.vector.tensor_scalar(b2_gb[:], mod[:, 5], b2_sum[:], None, ALU.mult).then_inc(mod_done, 1)
            dve.wait_ge(a_rstd_done, 2)
            normalise(1, 1)
            statistics(2)
            dve.wait_ge(low_mm, 1)
            nc.vector.tensor_copy(m_dt[:], bank[:, 3, 0:D]).then_inc(low_done, 1)
            nc.vector.tensor_copy(m_c[:], bank[:, 3, D:2 * D]).then_inc(low_done, 1)
            dve.wait_ge(ld_ident, 16)
            nc.vector.tensor_copy(ident_bf[:], ident_sb[:]).then_inc(ident_done, 1)
            for b in range(0, BATCH, 2):
                group = b // 2 + 2
                if b + 2 < BATCH:
                    dve.wait_ge(a_rstd_done, group + 1)
                    normalise(b + 2, 0)
                convolve(b, 0)
                if b + 4 < BATCH:
                    statistics(group + 1)
                convolve(b + 1, 1)
            b_low(0, 0, bank[:, 2])
            dt_sum(0, 0)
            dve.wait_ge(dt_done, 1)
            nc.vector.tensor_tensor(u_two[:, 0], dt_two[:, 0], seq(xs_all, 0), ALU.mult).then_inc(u_done, 1)

            def step(i, par):
                on = stages(i)
                p, j, f = i + 1, i - 1, i - 2
                for k in range(UNITS):
                    pair = bank[:, PER_UNIT * (k % 2):PER_UNIT * (k % 2) + PER_UNIT]
                    if on["scan"]:
                        if k == 0:
                            dve.wait_ge(u_done, i + 1)
                        dve.wait_ge(b_cast, UNITS * i + k + 1)
                        u_rep = u_two[:, par].unsqueeze(1).to_broadcast([128, PER_UNIT, T])
                        nc.vector.tensor_tensor(pair, pair, u_rep, ALU.mult).then_inc(bu_done, 1)
                    if k == 1 and on["mix"]:
                        dve.wait_ge(c_copied, j + 1)
                        dve.wait_ge(sum_done, j + 1)
                        nc.vector.tensor_tensor(y_sb, seq(c_all, j), s_sum[:], ALU.mult).then_inc(cs_done, 1)
                        dve.wait_ge(cs_done, j + 1)
                        nc.vector.scalar_tensor_tensor(y_sb, seq(xs_all, j), col("d"), y_sb,
                                                       ALU.mult, ALU.add).then_inc(y_done, 1)
                    if k == 2 and on["mix"]:
                        dve.wait_ge(o_mm, j + 1)
                        nc.vector.scalar_tensor_tensor(attn, misc, mod[:, 2, bass.ds(j, 1)], seq(zs_all, j),
                                                       ALU.mult, ALU.mult).then_inc(attn_done, 1)
                    if k == 5 and on["prepare"]:
                        b_low(p, 1 - par, misc)
                    if k == 4 and on["mix"]:
                        dve.wait_ge(x2_tok_done, j + 1)
                        for c in range(CHUNKS):
                            nc.vector.bn_stats(b_stats[:, c], x2_tok[:, c]).then_inc(b_stats_done, 1)
                        dve.wait_ge(b_stats_done, CHUNKS * j + CHUNKS)
                        nc.vector.tensor_tensor(mean_two[:], b_stats[:, :, 1], b_stats[:, :, 4], ALU.add).then_inc(b_mv_done, 1)
                        for c in range(CHUNKS):
                            nc.vector.bn_aggr(b_mv[:, c], b_stats[:, c]).then_inc(b_mv_done, 1)
                    if k == 5 and on["prepare"]:
                        dt_sum(p, 1 - par)
                    if k == 7 and on["mix"]:
                        scores = misc[:, 0:EXPERTS * CHUNKS].rearrange("p (c e) -> p c e", e=EXPERTS)
                        dve.wait_ge(gate_mm, j + 1)
                        nc.vector.tensor_reduce(g_max[:], scores, AX, ALU.max).then_inc(gate_dve, 1)
                        dve.wait_ge(gate_dve, 6 * j + 1)
                        nc.vector.tensor_tensor(g_sub[:], scores, g_max[:].unsqueeze(2).to_broadcast([128, CHUNKS, EXPERTS]),
                                                ALU.subtract).then_inc(gate_dve, 1)
                    if on["scan"]:
                        dve.wait_ge(bu_done, UNITS * i + k + 1)
                        dve.wait_ge(decay_done, UNITS * i + k + 1)
                        n = units_released(i, k)
                        if not isinstance(i, int) or UNITS * i + k >= RING:
                            dve.wait_ge(units_added, n)
                        nc.vector.tensor_tensor_scan(
                            s_ring[:, k % RING].rearrange("p s t -> p (s t)"),
                            a_ring[:, k % RING].rearrange("p s t -> p (s t)"),
                            pair.rearrange("p s t -> p (s t)"), 0.0, ALU.mult, ALU.add).then_inc(scan_done, 1)
                    if k == 0 and on["experts"]:
                        dve.wait_ge(mask_mm, f + 1)
                        nc.vector.tensor_tensor(h2[:, 1], mask_bank(par), h2[:, 0],
                                                ALU.mult).then_inc(first_done, 1)
                    if k == 7 and on["mix"]:
                        dve.wait_ge(gate_exp, j + 1)
                        nc.vector.tensor_reduce(g_den[:], g_exp[:], AX, ALU.add).then_inc(gate_dve, 1)
                        dve.wait_ge(gate_dve, 6 * j + 3)
                        nc.vector.reciprocal(g_inv[:], g_den[:]).then_inc(gate_dve, 1)
                        dve.wait_ge(gate_dve, 6 * j + 4)
                        nc.vector.tensor_tensor(g_prob[:], g_exp[:], g_inv[:].unsqueeze(2).to_broadcast([128, CHUNKS, EXPERTS]),
                                                ALU.mult).then_inc(gate_dve, 1)
                        dve.wait_ge(gate_dve, 6 * j + 5)
                        nc.vector.tensor_tensor(g_first[:], g_prob[:, :, 0], g_prob[:, :, 1], ALU.is_ge).then_inc(gate_dve, 1)
                if on["experts"] and not on["scan"]:
                    add_residual(dve, nc.vector, f, par)

            run_steps(dve, step)

        @block.gpsimd
        def _(pool):
            pool.wait_ge(consts_set, 4)

            def rstd(n):
                first, end = GROUPS[n]
                g = slice(CHUNKS * first, CHUNKS * end)
                pool.wait_ge(a_sum_done, 3 * n + 3)
                nc.gpsimd.tensor_tensor(a_rstd[:, g], a_var[:, g], half_neg[:, g], ALU.pow).then_inc(a_rstd_done, 1)

            def normalise(n):
                b = 2 * n + 3
                tokens = bass.ds(CHUNKS * b, CHUNKS)
                pool.wait_ge(a_xt_done, 2 * n + 2)
                nc.gpsimd.tensor_tensor(x_norm[:, 1], x_tok[:].rearrange("p b c d -> p (b c) d")[:, tokens],
                                        a_mean[:, tokens].unsqueeze(2).to_broadcast([128, CHUNKS, D]),
                                        ALU.subtract).then_inc(a_norm_pool, 1)
                pool.wait_ge(a_norm_pool, 2 * n + 1)
                nc.gpsimd.tensor_tensor(x_norm[:, 1], x_norm[:, 1],
                                        a_rstd[:, tokens].unsqueeze(2).to_broadcast([128, CHUNKS, D]),
                                        ALU.mult).then_inc(a_norm_pool, 1)

            rstd(0)
            rstd(1)
            for group in range(2, len(GROUPS)):
                rstd(group)
                pool.wait_ge(a_rstd_done, group + 1)
                normalise(group - 2)

            def make_u(p, par):
                pool.wait_ge(dt_done, p + 1)
                nc.gpsimd.tensor_tensor(u_two[:, par], dt_two[:, par], seq(xs_all, p), ALU.mult).then_inc(u_done, 1)

            pool.wait_ge(ld_xT, 16)

            def step(i, par):
                on = stages(i)
                p, j, f = i + 1, i - 1, i - 2
                for k in range(UNITS):
                    if k == 4 and on["mix"]:
                        pool.wait_ge(b_mv_done, (CHUNKS + 1) * (j + 1))
                        if not isinstance(j, int) or j > 0:
                            pool.wait_ge(b_norm_done, CHUNKS * j)
                        nc.gpsimd.tensor_tensor(b_var[:], b_mv[:, :, 1], eps_row[:], ALU.add)
                        nc.gpsimd.tensor_tensor(neg_mean[:], mean_two[:], half_neg[:, 0:CHUNKS], ALU.mult).then_inc(b_var_done, 1)
                        pool.wait_ge(b_var_done, j + 1)
                        nc.gpsimd.tensor_tensor(b_rstd[:], b_var[:], half_neg[:, 0:CHUNKS], ALU.pow).then_inc(b_rstd_done, 1)
                        pool.wait_ge(b_rstd_done, 2 * j + 1)
                        nc.gpsimd.tensor_tensor(b_shift[:], neg_mean[:], b_rstd[:], ALU.mult).then_inc(b_rstd_done, 1)
                    if k == 2 and on["mix"]:
                        pool.wait_ge(attn_done, j + 1)
                        if not isinstance(j, int) or j > 1:
                            pool.wait_ge(out_done, j - 1)
                        nc.gpsimd.tensor_tensor(x2_two[:, 1 - par].rearrange("p c t -> p (c t)"), attn, seq(x_res, j),
                                                ALU.add).then_inc(x2_done, 1)
                    if on["scan"] and k:
                        pool.wait_ge(scan_done, UNITS * i + k + 1)
                        n = ADDS * i + k - 1
                        if not isinstance(i, int) or n > 0:
                            pool.wait_ge(units_added, n)
                        if k == 1 and (not isinstance(i, int) or i > 0):
                            pool.wait_ge(sum_done, i)
                        into = s_ring[:, 0] if k == 1 else s_acc[:]
                        nc.gpsimd.tensor_tensor(s_acc[:], into, s_ring[:, k % RING], ALU.add).then_inc(units_added, 1)
                    if k == 0 and on["experts"]:
                        pool.wait_ge(first_done, f + 1)
                        nc.gpsimd.tensor_tensor(h2[:, 2], h2[:, 0], h2[:, 1], ALU.subtract).then_inc(second_done, 1)
                    if k == 5 and on["prepare"]:
                        make_u(p, 1 - par)
                if on["scan"]:
                    pool.wait_ge(units_added, ADDS * i + ADDS)
                    if not isinstance(i, int) or i > 0:
                        pool.wait_ge(cs_done, i)
                    nc.gpsimd.tensor_tensor(s_sum[:], s_acc[:, 0], s_acc[:, 1], ALU.add).then_inc(sum_done, 1)
                if on["experts"] and on["scan"]:
                    add_residual(pool, nc.gpsimd, f, par)

            run_steps(pool, step)


def kernel(**inputs):
    import concourse.bacc as bacc
    from concourse.bass_utils import run_bass_kernel_spmd

    g = {k: np.asarray(v) for k, v in inputs.items()}

    def put(a):
        return np.ascontiguousarray(a)

    x = g["L0_attn_x"]
    w_x = g["L0_attn_W_x"]
    zeros = np.zeros((D, HALF - STATES), np.float32)
    b_rows = w_x[RANK:RANK + STATES].T
    w_c_pad = np.zeros((RANK, 2 * D), np.float32)
    w_c_pad[:STATES, :D] = w_x[RANK + STATES:]
    w_c_pad[:STATES, D:] = g["L0_attn_W_C"].T
    w1 = np.stack([g["L0_ffn_sw1"], *g["L0_ffn_w1"]], 1)
    w2 = np.stack([g["L0_ffn_sw2"], *g["L0_ffn_w2"]], 0)
    b1 = np.stack([g["L0_ffn_sb1"], *g["L0_ffn_b1"]], 0)
    b2 = np.stack([g["L0_ffn_sb2"], *g["L0_ffn_b2"]], 0)
    sel = np.zeros((128, STATES), np.float32)
    for n in range(STATES):
        sel[n, n] = sel[HALF + n, n] = 1.0
    arrays = {
        "x": x,
        "xT": x.reshape(BATCH * T, D).T,
        "cols": np.concatenate([g["L0_attn_conv_w"], g["L0_attn_b_dt"][:, None], g["L0_attn_A_log"],
                                g["L0_attn_D_param"][:, None], b1.reshape(TILES, 128).T, b2.T, g["L0_c"].T,
                                g["L0_ffn_gate_w"].T], 1),
        "wsq": np.concatenate([g["L0_attn_W_in"].T, g["L0_attn_W_out"].T, b_rows, zeros, b_rows, zeros,
                               np.zeros((D, 128 - 2 * HALF), np.float32)], 1),
        "wmod": g["L0_wmod"],
        "wlow": np.concatenate([w_x[:RANK], g["L0_attn_W_dt"].T, w_c_pad], 1),
        "w1": w1,
        "w2": w2.reshape(NETS, HCH, 128, D).transpose(2, 0, 1, 3),
        "sel": sel,
        "ident": np.eye(128, dtype=np.float32),
    }
    nc = bacc.Bacc("TRN2", target_bir_lowering=False, num_devices=1)
    arrays = {f"in_{k}": put(v) for k, v in arrays.items()}
    aps = [nc.dram_tensor(k, v.shape, mybir.dt.from_np(v.dtype), kind="ExternalInput").ap() for k, v in arrays.items()]
    outT = nc.dram_tensor("outT", (D, BATCH * T), FP32, kind="ExternalOutput").ap()
    adaln_kernel(nc, *aps, outT)
    r = run_bass_kernel_spmd(nc, [arrays], core_ids=[0])
    return put(r.results[0]["outT"].reshape(D, BATCH, T).transpose(1, 2, 0))
```
